# Optimizing a Trainium2 kernel written in Bass

```python
import numpy as np
import jax
import jax.numpy as jnp

def _softmax(x, axis=-1):
    return jax.nn.softmax(x, axis=axis)

def _gelu(x):
    return jax.nn.gelu(x, approximate=True)

def _silu(x):
    return jax.nn.silu(x)

def _sigmoid(x):
    return jax.nn.sigmoid(x)

def _layernorm(x, axis=-1, eps=1e-05):
    m = jnp.mean(x, axis=axis, keepdims=True)
    v = jnp.var(x, axis=axis, keepdims=True)
    return (x - m) / jnp.sqrt(v + eps)

def _scatter_add(tgt, idx, src, axis=0):
    return tgt.at[idx].add(src)

def _segment_sum(src, seg, n):
    return jax.ops.segment_sum(src, seg, n)
kernel_name = 'mk_metaformer_d1_conv_nchw768_r4_69ce9d'

def setup_inputs(seed: int=0):
    np.random.seed(seed)
    _w = jnp.asarray

    def _rec_inputs():
        import jax
        import jax.numpy as jnp
        _gk = jax.random.key(seed)
        x = -0.0002221 + 1 * jax.random.normal(jax.random.fold_in(_gk, 1), (8, 192, 16, 16), jnp.float32)
        return x
    x = _rec_inputs()

    def _L0_conv_setup():
        import jax, jax.numpy as jnp
        import numpy as np
        CHUNK = 16

        def l2norm(x, eps=1e-06):
            return x * jax.lax.rsqrt(jnp.sum(x * x, axis=-1, keepdims=True) + eps)

        def delta_rule_chunked(q, k, v, beta):
            B, H, L, D = q.shape
            n = L // CHUNK

            def to_chunks(t):
                return jnp.moveaxis(t.reshape(B, H, n, CHUNK, *(t.shape[4:] if t.ndim > 4 else ())) if False else t.reshape(B, H, n, CHUNK, -1) if t.ndim == 4 else t.reshape(B, H, n, CHUNK), 2, 0)
            qc = jnp.moveaxis(q.reshape(B, H, n, CHUNK, D), 2, 0)
            kc = jnp.moveaxis(k.reshape(B, H, n, CHUNK, D), 2, 0)
            vc = jnp.moveaxis(v.reshape(B, H, n, CHUNK, D), 2, 0)
            bc = jnp.moveaxis(beta.reshape(B, H, n, CHUNK), 2, 0)
            strict = jnp.tril(jnp.ones((CHUNK, CHUNK), bool), -1)
            incl = jnp.tril(jnp.ones((CHUNK, CHUNK), bool))
            eye = jnp.eye(CHUNK, dtype=q.dtype)

            def step(S, inp):
                qi, ki, vi, bi = inp
                kk = jnp.einsum('bhid,bhjd->bhij', ki, ki)
                T = eye + jnp.where(strict, bi[..., :, None] * kk, 0.0)
                rhs = bi[..., None] * (vi - jnp.einsum('bhcd,bhde->bhce', ki, S))
                U = jax.scipy.linalg.solve_triangular(T, rhs, lower=True)
                qk = jnp.einsum('bhid,bhjd->bhij', qi, ki)
                O = jnp.einsum('bhcd,bhde->bhce', qi, S) + jnp.einsum('bhij,bhje->bhie', jnp.where(incl, qk, 0.0), U)
                S_new = S + jnp.einsum('bhcd,bhce->bhde', ki, U)
                return (S_new, O)
            S0 = jnp.zeros((B, H, D, D), q.dtype)
            _, O = jax.lax.scan(step, S0, (qc, kc, vc, bc))
            return jnp.moveaxis(O, 0, 2).reshape(B, H, L, D)
        key = jax.random.key(seed)
        ks = jax.random.split(key, 7)
        B, C, Hh, Ww = (8, 192, 16, 16)
        n_heads = 12
        s = 1.0 / np.sqrt(C)
        x = jax.random.normal(ks[0], (B, C, Hh, Ww), jnp.float32)
        Wq = jax.random.normal(ks[1], (C, C), jnp.float32) * s
        Wk = jax.random.normal(ks[2], (C, C), jnp.float32) * s
        Wv = jax.random.normal(ks[3], (C, C), jnp.float32) * s
        Wb = jax.random.normal(ks[4], (C, n_heads), jnp.float32) * s
        Wo = jax.random.normal(ks[5], (C, C), jnp.float32) * s
        return {'x': x, 'Wq': Wq, 'Wk': Wk, 'Wv': Wv, 'Wb': Wb, 'Wo': Wo}
    _L0_conv_all = _L0_conv_setup()
    _L0_conv_in = {k: v for k, v in _L0_conv_all.items() if k in ('Wq', 'Wk', 'Wv', 'Wb', 'Wo')}
    del _L0_conv_all

    def _L0_ffn_setup():
        import jax, jax.numpy as jnp
        import numpy as np
        B, S, D = (4, 256, 192)
        E = 8
        H = 192
        HS = 768
        TOPK_ROUTED = 2
        key = jax.random.key(seed)
        ks = jax.random.split(key, 10)
        w = lambda k, shape: jax.random.normal(k, shape, dtype=jnp.float32) * 0.02
        return {'x': jax.random.normal(ks[0], (B, S, D), dtype=jnp.float32), 'router_w': w(ks[1], (D, E)), 'w_gate': w(ks[2], (E, D, H)), 'w_up': w(ks[3], (E, D, H)), 'w_down': w(ks[4], (E, H, D)), 'ws_gate': w(ks[5], (D, HS)), 'ws_up': w(ks[6], (D, HS)), 'ws_down': w(ks[7], (HS, D)), 'sg_w': w(ks[8], (D, 1)), 'sg_b': jnp.zeros((1,), jnp.float32)}
    _L0_ffn_all = _L0_ffn_setup()
    _L0_ffn_in = {k: v for k, v in _L0_ffn_all.items() if k in ('router_w', 'w_gate', 'w_up', 'w_down', 'ws_gate', 'ws_up', 'ws_down', 'sg_w', 'sg_b')}
    del _L0_ffn_all
    return {'x': x, 'L0_conv_Wq': _L0_conv_in['Wq'], 'L0_conv_Wk': _L0_conv_in['Wk'], 'L0_conv_Wv': _L0_conv_in['Wv'], 'L0_conv_Wb': _L0_conv_in['Wb'], 'L0_conv_Wo': _L0_conv_in['Wo'], 'L0_ffn_router_w': _L0_ffn_in['router_w'], 'L0_ffn_w_gate': _L0_ffn_in['w_gate'], 'L0_ffn_w_up': _L0_ffn_in['w_up'], 'L0_ffn_w_down': _L0_ffn_in['w_down'], 'L0_ffn_ws_gate': _L0_ffn_in['ws_gate'], 'L0_ffn_ws_up': _L0_ffn_in['ws_up'], 'L0_ffn_ws_down': _L0_ffn_in['ws_down'], 'L0_ffn_sg_w': _L0_ffn_in['sg_w'], 'L0_ffn_sg_b': _L0_ffn_in['sg_b']}

def reference(x, L0_conv_Wq, L0_conv_Wk, L0_conv_Wv, L0_conv_Wb, L0_conv_Wo, L0_ffn_router_w, L0_ffn_w_gate, L0_ffn_w_up, L0_ffn_w_down, L0_ffn_ws_gate, L0_ffn_ws_up, L0_ffn_ws_down, L0_ffn_sg_w, L0_ffn_sg_b):
    import jax
    import jax.numpy as jnp

    def _L0_conv_ref(x, Wq, Wk, Wv, Wb, Wo):
        import jax, jax.numpy as jnp
        import numpy as np
        CHUNK = 16

        def l2norm(x, eps=1e-06):
            return x * jax.lax.rsqrt(jnp.sum(x * x, axis=-1, keepdims=True) + eps)

        def delta_rule_chunked(q, k, v, beta):
            B, H, L, D = q.shape
            n = L // CHUNK

            def to_chunks(t):
                return jnp.moveaxis(t.reshape(B, H, n, CHUNK, *(t.shape[4:] if t.ndim > 4 else ())) if False else t.reshape(B, H, n, CHUNK, -1) if t.ndim == 4 else t.reshape(B, H, n, CHUNK), 2, 0)
            qc = jnp.moveaxis(q.reshape(B, H, n, CHUNK, D), 2, 0)
            kc = jnp.moveaxis(k.reshape(B, H, n, CHUNK, D), 2, 0)
            vc = jnp.moveaxis(v.reshape(B, H, n, CHUNK, D), 2, 0)
            bc = jnp.moveaxis(beta.reshape(B, H, n, CHUNK), 2, 0)
            strict = jnp.tril(jnp.ones((CHUNK, CHUNK), bool), -1)
            incl = jnp.tril(jnp.ones((CHUNK, CHUNK), bool))
            eye = jnp.eye(CHUNK, dtype=q.dtype)

            def step(S, inp):
                qi, ki, vi, bi = inp
                kk = jnp.einsum('bhid,bhjd->bhij', ki, ki)
                T = eye + jnp.where(strict, bi[..., :, None] * kk, 0.0)
                rhs = bi[..., None] * (vi - jnp.einsum('bhcd,bhde->bhce', ki, S))
                U = jax.scipy.linalg.solve_triangular(T, rhs, lower=True)
                qk = jnp.einsum('bhid,bhjd->bhij', qi, ki)
                O = jnp.einsum('bhcd,bhde->bhce', qi, S) + jnp.einsum('bhij,bhje->bhie', jnp.where(incl, qk, 0.0), U)
                S_new = S + jnp.einsum('bhcd,bhce->bhde', ki, U)
                return (S_new, O)
            S0 = jnp.zeros((B, H, D, D), q.dtype)
            _, O = jax.lax.scan(step, S0, (qc, kc, vc, bc))
            return jnp.moveaxis(O, 0, 2).reshape(B, H, L, D)
        B, C, Hh, Ww = x.shape
        L = Hh * Ww
        n_heads = Wb.shape[1]
        D = C // n_heads
        t = x.reshape(B, C, L).transpose(0, 2, 1)

        def heads(z):
            return z.reshape(B, L, n_heads, D).transpose(0, 2, 1, 3)
        q = l2norm(heads(jax.nn.silu(t @ Wq)))
        k = l2norm(heads(jax.nn.silu(t @ Wk)))
        v = heads(jax.nn.silu(t @ Wv))
        beta = jax.nn.sigmoid(t @ Wb).transpose(0, 2, 1)
        o = delta_rule_chunked(q, k, v, beta)
        o = o.transpose(0, 2, 1, 3).reshape(B, L, C)
        y = o @ Wo
        out = t + y
        return out.transpose(0, 2, 1).reshape(B, C, Hh, Ww)

    def _L0_ffn_ref(x, router_w, w_gate, w_up, w_down, ws_gate, ws_up, ws_down, sg_w, sg_b):
        import jax, jax.numpy as jnp
        import numpy as np
        B, S, D = (4, 256, 192)
        E = 8
        H = 192
        HS = 768
        TOPK_ROUTED = 2
        probs = jax.nn.softmax(x @ router_w, axis=-1)
        gates, idx = jax.lax.top_k(probs, TOPK_ROUTED)
        gates = gates / jnp.sum(gates, axis=-1, keepdims=True)
        n_exp = router_w.shape[1]
        dense_g = jnp.sum(jax.nn.one_hot(idx, n_exp, dtype=x.dtype) * gates[..., None], axis=-2)
        g = jax.nn.silu(jnp.einsum('bsd,edh->bseh', x, w_gate))
        u = jnp.einsum('bsd,edh->bseh', x, w_up)
        expert_out = jnp.einsum('bseh,ehd->bsed', g * u, w_down)
        routed = jnp.einsum('bse,bsed->bsd', dense_g, expert_out)
        shared = jax.nn.silu(x @ ws_gate) * (x @ ws_up) @ ws_down
        alpha = jax.nn.sigmoid(x @ sg_w + sg_b)
        return alpha * shared + (1.0 - alpha) * routed

    def _gn(v, G=32, eps=1e-05):
        B_, C_, H_, W_ = v.shape
        g = v.reshape(B_, G, C_ // G, H_, W_)
        m = jnp.mean(g, axis=(2, 3, 4), keepdims=True)
        s = jnp.var(g, axis=(2, 3, 4), keepdims=True)
        return ((g - m) / jnp.sqrt(s + eps)).reshape(v.shape)

    def _ln_c(v, eps=1e-06):
        m = jnp.mean(v, axis=1, keepdims=True)
        s = jnp.var(v, axis=1, keepdims=True)
        return (v - m) / jnp.sqrt(s + eps)

    def _ln_t(v, eps=1e-05):
        m = jnp.mean(v, axis=-1, keepdims=True)
        s = jnp.var(v, axis=-1, keepdims=True)
        return (v - m) / jnp.sqrt(s + eps)

    def _to_tokens(v):
        B_, C_, H_, W_ = v.shape
        return v.reshape(B_, C_, H_ * W_).transpose(0, 2, 1)

    def _from_tokens(t, like):
        B_, C_, H_, W_ = like.shape
        return t.transpose(0, 2, 1).reshape(B_, C_, H_, W_)
    x = x + _L0_conv_ref(_ln_c(x), L0_conv_Wq, L0_conv_Wk, L0_conv_Wv, L0_conv_Wb, L0_conv_Wo)
    t = _to_tokens(x)
    t = t + _L0_ffn_ref(_ln_t(t), L0_ffn_router_w, L0_ffn_w_gate, L0_ffn_w_up, L0_ffn_w_down, L0_ffn_ws_gate, L0_ffn_ws_up, L0_ffn_ws_down, L0_ffn_sg_w, L0_ffn_sg_b)
    x = _from_tokens(t, x)
    return x

_drawn_inputs = setup_inputs


def setup_inputs(seed=0):
    import zlib

    import numpy as np

    out = dict(_drawn_inputs(seed))
    spreads = {}
    factors = {'L0_ffn_router_w': 8.0,
     'L0_ffn_w_gate': 8.0,
     'L0_ffn_w_up': 8.0,
     'L0_ffn_w_down': 8.0,
     'L0_ffn_ws_gate': 8.0,
     'L0_ffn_ws_up': 8.0,
     'L0_ffn_ws_down': 8.0,
     'L0_ffn_sg_w': 8.0}
    for name, (base, spread) in spreads.items():
        noise = np.random.default_rng([zlib.crc32(name.encode()), seed]).standard_normal(out[name].shape)
        drawn = base * np.exp(spread * noise) if base else spread * noise
        out[name] = jnp.asarray(drawn.astype(out[name].dtype))
    for name, factor in factors.items():
        out[name] = (out[name] * factor).astype(out[name].dtype)
    return out
```

```python
import concourse.bass as bass
from concourse import mybir
from contextlib import ExitStack

F32 = mybir.dt.float32
ALU = mybir.AluOpType
ACT = mybir.ActivationFunctionType
X = mybir.AxisListType.X

NB, C, L = 8, 192, 256
NH, D = 12, 16
T = 16
NC = L // T
P = 128
C0, C1 = P, C - P
BP, BR, HP, HX = 4, 2, 6, 2
G = HP * D
E, H, HS = 8, 192, 768
UN = E + HS // H
HID = UN * H
KT = HID // P
GRP = [(0, 4), (4, 8), (8, 12), (12, 16), (16, 18)]
NG = len(GRP)
RING = 4
NQK, NVB = 2 * C, C + NH


def build(nc, x, Wq, Wk, Wv, Wb, Wo, router_w, w_gate, w_up, w_down, ws_gate, ws_up, ws_down, sg_w, sg_b, out):
    ctx = ExitStack()
    with ctx:
        def sb(name, shape):
            return ctx.enter_context(nc.sbuf_tensor(name, shape, F32))

        def sem(name):
            return ctx.enter_context(nc.semaphore(name))

        kq_dram = nc.dram_tensor("kq_scratch", [NC, 2, BP, HX, BR * T, G], F32, kind="Internal").ap()

        xT0 = sb("xT0", [C0, NB, L])
        low = sb("low", [P, UN * 2 * H])
        xT1 = low[C1:P, 0:NB * L].rearrange("c (b l) -> c b l", b=NB)
        ident = sb("ident", [P, P])
        Wp0, Wp1 = sb("Wp0", [C0, NQK + NVB]), sb("Wp1", [C1, NQK + NVB])
        Wo0, Wo1 = sb("Wo0", [C0, C]), sb("Wo1", [C1, C])
        Wr0, Wr1 = sb("Wr0", [C0, E + 1]), sb("Wr1", [C1, E + 1])
        Wu0 = sb("Wu0", [C0, UN, 2 * H])
        Wu1 = low[0:C1, :].rearrange("c (n h) -> c n h", n=UN)
        Wd = sb("Wd", [P, KT, C])
        xh = sb("xh", [P, NC, C])
        neg_half, eps6, eps5, one = sb("neg_half", [P, 1]), sb("eps6", [P, 1]), sb("eps5", [P, 1]), sb("one", [P, 1])
        sgb, neg_sgb = sb("sgb", [P, 1]), sb("neg_sgb", [P, 1])
        lower = sb("lower", [P, E, E])
        xs0, xs = sb("xs0", [C0, NB, T]), sb("xs1", [P, NB, T])
        xs1 = xs[C1:P]
        st1, mv1 = sb("st1", [P, 6]), sb("mv1", [P, 2])
        ve1, rstd1, nmr1 = sb("ve1", [P, 1]), sb("rstd1", [P, 1]), sb("nmr1", [P, 1])
        h = sb("h", [P, C])
        hT0, hT1 = sb("hT0", [C0, P]), sb("hT1", [C1, P])
        zc = sb("zc", [P, NH])
        qk = sb("qk", [P, 2, HX, HP, D])
        sq = sb("sq", [P, 2, HX, HP, D])
        v = sb("v", [P, HP, HX, D])
        ss, ez, lns, inv = sb("ss", [P, 24]), sb("ez", [P, NH]), sb("lns", [P, 36]), sb("inv", [P, 36])
        ksc = sb("ksc", [P, HX, HP])
        kqn = sb("kqn", [P, 2, HX, G])
        vn = sb("vn", [P, HP, HX, D])
        vT = sb("vT", [P, 2, HP, BR, T])
        KB = sb("KB", [P, 2, BR, T, HP, D])
        QB = sb("QB", [P, 2, BR, T, HP, D])
        Pr = sb("Pr", [P, BR, T, HP, D + 1])
        u = sb("u", [P, 2, BR, HP])
        TT = sb("TT", [P, 2, BR, HP, D])
        SH = sb("SH", [P, 2, T, BR, HP, D])
        PQ = sb("PQ", [P, T // 2 * BR * HP, D])
        oT = sb("oT", [P, HP, BR, T])
        otok = sb("otok", [P, C])
        oc0, oc1 = sb("oc0", [C0, P]), sb("oc1", [C1, P])
        st2, mv2 = sb("st2", [P, 6]), sb("mv2", [P, 2])
        ve2, rstd2, nmr2 = sb("ve2", [P, 1]), sb("rstd2", [P, 1]), sb("nmr2", [P, 1])
        h2 = sb("h2", [P, C])
        h2T0, h2T1 = sb("h2T0", [C0, 2, P]), sb("h2T1", [C1, 2, P])
        negmax, prob = sb("negmax", [P, 1]), sb("prob", [P, E + 1])
        gt, eq, rank = sb("gt", [P, E, E]), sb("eq", [P, E, E]), sb("rank", [P, E])
        sel, den, rden, coef = sb("sel", [P, E]), sb("den", [P, 2]), sb("rden", [P, 2]), sb("coef", [P, 1])
        gate = sb("gate", [P, 2, UN])
        sg, ug = sb("sg", [P, RING, H]), sb("ug", [P, RING, H])
        hid = sb("hid", [P, HID])
        hidT = sb("hidT", [P, 2, 4, P])
        res = sb("res", [P, C])

        bank = [ctx.enter_context(nc.psum_tensor(f"bank{i}", [P, 512], F32)) for i in range(8)]
        bA, bQK, bFa, bDn = bank[0], bank[1], bank[2], bank[3]
        bUp, bHt = bank[4:6], bank[6:8]

        s_x, s_wp, s_wo, s_wr, s_wu, s_wd = (sem(n) for n in ("x_in", "wp_in", "wo_in", "wr_in", "wu_in", "wd_in"))
        s_const, s_zero, s_id, s_low = sem("consts_ready"), sem("state_zero"), sem("ident_ready"), sem("lower_ready")
        s_sgb = sem("sgb_ready")
        s_chain = sem("dve_chain")
        s_pool = sem("pool_chain")
        s_act = sem("act_chain")
        s_xs, s_xT, s_st1, s_rs1, s_nm1, s_h, s_xh = (sem(n) for n in (
            "xs_ready", "xT_ready", "stats1_ready", "rstd1_ready", "nmr1_ready", "h_ready", "xh_ready"))
        s_hTp, s_hT, s_qk, s_vb, s_z, s_qks, s_vs, s_sq, s_ss, s_inv = (sem(n) for n in (
            "hT_psum_ready", "hT_ready", "qk_ready", "vb_ready", "z_ready", "qk_silu_ready", "v_silu_ready",
            "squares_ready", "norms_ready", "inv_ready"))
        s_kn, s_qn, s_vn, s_vT, s_place = (sem(n) for n in (
            "k_normed", "q_normed", "v_normed", "vT_ready", "v_placed"))
        s_scr = sem("scratch_written")
        s_KB, s_QB = [sem("KB_in_even"), sem("KB_in_odd")], [sem("QB_in_even"), sem("QB_in_odd")]
        s_state, s_pq, s_oT = sem("states_ready"), sem("states_read"), sem("o_summed")
        s_otok, s_ocp, s_oc, s_y, s_st2, s_rs2, s_nm2, s_h2 = (sem(n) for n in (
            "o_by_token", "oc_psum_ready", "oc_ready", "y_ready", "stats2_ready", "rstd2_ready", "nmr2_ready", "h2_ready"))
        s_h2Tp, s_h2T, s_lg, s_nmx, s_pr, s_gate = (sem(n) for n in (
            "h2T_psum_ready", "h2T_ready", "logits_ready", "negmax_ready", "probs_ready", "gates_ready"))
        s_up, s_ug, s_hid = sem("up_ready"), sem("unit_copied"), sem("hidden_ready")
        s_ht, s_htc, s_dg = sem("hidT_psum_ready"), sem("hidT_ready"), sem("down_group_done")
        s_res, s_outp, s_outc, s_out = sem("res_ready"), sem("outT_psum_ready"), sem("out_copied"), sem("out_written")

        block = ctx.enter_context(nc.Block())

        def chunks(eng, prologue, step):
            prologue()

            def it(c, par):
                step(c, par, dict(A=c + 2, A2=c + 1, R=c, Fa=c - 1, Fb=c - 2, Fc=c - 3))
            def edge(c):
                on = dict(A=c + 2, A2=c + 1, R=c, Fa=c - 1, Fb=c - 2, Fc=c - 3)
                step(c, c % 2, {k: n for k, n in on.items() if 0 <= n < NC})
            for c in range(4):
                edge(c)
            with eng.Fori(0, 5) as k:
                for j in range(2):
                    it(eng.snap(k * 2 + (4 + j)), j)
            for c in range(14, NC + 3):
                edge(c)

        def turn_bank(g):
            return g % 2

        def loads(c, par):
            return c * 8 + (16 - 8 * par)

        def old(w, n):
            return not isinstance(n, int) or n >= 0

        @block.sync
        def _(sp):
            def scratch(a):
                sp.wait_ge(s_kn, a + 1)
                sp.wait_ge(s_qn, a + 1)
                for t in range(2):
                    for bp in range(BP):
                        sp.dma_start(kq_dram[bass.ds(a, 1), t, bp].rearrange("z x r g -> r (z x) g"),
                                     kqn[32 * bp:32 * bp + 32, t]).then_inc(s_scr, 16)

            def spread(a, par):
                sp.wait_ge(s_scr, (a + 1) * 128)
                if old(0, a if not isinstance(a, int) else a - 2):
                    sp.wait_ge(s_state, a * 2 - 2)
                sp.dma_start(KB[:, par].rearrange("p b i h d -> p (b i h d)"),
                             kq_dram[bass.ds(a, 1), 0].rearrange("z b x r g -> (z b x) (r g)").unsqueeze(1).to_broadcast(
                                 [BP * HX, D, BR * T * G])).then_inc(s_KB[par], 16)
                if old(0, a if not isinstance(a, int) else a - 2):
                    sp.wait_ge(s_pq, a * 2 - 2)
                sp.dma_start(QB[:, par].rearrange("p b i h d -> p (b i h d)"),
                             kq_dram[bass.ds(a, 1), 1].rearrange("z b x r g -> (z b x) (r g)").unsqueeze(1).to_broadcast(
                                 [BP * HX, D, BR * T * G])).then_inc(s_QB[par], 16)

            def prologue():
                sp.dma_start(xT0[:, :, :], x[:, 0:C0].rearrange("b c l -> c b l")).then_inc(s_x, 16)
                sp.dma_start(xT1[:, :, :], x[:, C0:C].rearrange("b c l -> c b l")).then_inc(s_x, 16)
                for i, w in enumerate((Wq, Wk, Wv)):
                    sp.dma_start(Wp0[:, i * C:i * C + C], w[0:C0, :]).then_inc(s_wp, 16)
                    sp.dma_start(Wp1[:, i * C:i * C + C], w[C0:C, :]).then_inc(s_wp, 16)
                sp.dma_start(Wp0[:, 3 * C:3 * C + NH], Wb[0:C0, :]).then_inc(s_wp, 16)
                sp.dma_start(Wp1[:, 3 * C:3 * C + NH], Wb[C0:C, :]).then_inc(s_wp, 16)
                scratch(0)
                spread(0, 0)
                sp.dma_start(Wo0[:, :], Wo[0:C0, :]).then_inc(s_wo, 16)
                sp.dma_start(Wo1[:, :], Wo[C0:C, :]).then_inc(s_wo, 16)
                sp.dma_start(Wr0[:, 0:E], router_w[0:C0, :]).then_inc(s_wr, 16)
                sp.dma_start(Wr1[:, 0:E], router_w[C0:C, :]).then_inc(s_wr, 16)
                sp.dma_start(Wr0[:, E:E + 1], sg_w[0:C0, :]).then_inc(s_wr, 16)
                sp.dma_start(Wr1[:, E:E + 1], sg_w[C0:C, :]).then_inc(s_wr, 16)
                sp.dma_start(sgb[:, :], sg_b.rearrange("(a n) -> a n", a=1).to_broadcast([P, 1])).then_inc(s_wr, 16)
                for half, we, ws in ((0, w_gate, ws_gate), (H, w_up, ws_up)):
                    for W, lo, hi in ((Wu0, 0, C0), (Wu1, C0, C)):
                        sp.dma_start(W[:, 0:E, half:half + H], we[:, lo:hi, :].rearrange("e c h -> c e h")).then_inc(s_wu, 16)
                        sp.dma_start(W[:, E:UN, half:half + H], ws[lo:hi, :].rearrange("c (s h) -> c s h", h=H)).then_inc(s_wu, 16)
                ke = E * H // P
                sp.dma_start(Wd[:, 0:ke, :], w_down.rearrange("e h c -> (e h) c").rearrange("(k p) c -> p k c", p=P)).then_inc(s_wd, 16)
                sp.dma_start(Wd[:, ke:KT, :], ws_down.rearrange("(k p) c -> p k c", p=P)).then_inc(s_wd, 16)
                scratch(1)

            def step(c, par, on):
                if "A2" in on:
                    spread(on["A2"], 1 - par)
                if "A" in on:
                    scratch(on["A"])

            chunks(sp, prologue, step)
            sp.wait_ge(s_outc, NC)
            sp.dma_start(out[:, 0:C0].rearrange("b c l -> c b l"), xT0[:, :, :]).then_inc(s_out, 16)
            sp.dma_start(out[:, C0:C].rearrange("b c l -> c b l"), xT1[:, :, :]).then_inc(s_out, 16)
            sp.wait_ge(s_out, 32)

        @block.tensor
        def _(pe):
            mm, tr = nc.tensor.matmul, nc.tensor.transpose

            def project(dst, a0, a1, w0, w1):
                mm(dst, a0, w0, start=True, stop=False)
                return mm(dst, a1, w1, start=False, stop=True)

            def turn(b, src):
                tr(b[:, 0:P], src[:, 0:C0], ident[:, :])
                return tr(b[0:C1, P:2 * P], src[:, C0:C], ident[:, :])

            def A_x(a):
                pe.wait_ge(s_xs, a + 1)
                if old(0, a if not isinstance(a, int) else a - 1):
                    pe.wait_ge(s_z, a)
                    pe.wait_ge(s_vs, a)
                tr(bA[:, 0:C0], xs0[:, :, :].rearrange("c b t -> c (b t)"), ident[:, :])
                tr(bA[:, C0:C], xs1.rearrange("c b t -> c (b t)"), ident[C1:P, C1:P]).then_inc(s_xT, 1)

            def A_h(a):
                pe.wait_ge(s_h, a + 1)
                pe.wait_ge(s_xh, a + 1)
                turn(bA, h).then_inc(s_hTp, 1)

            def A_proj(a, first=False):
                if first:
                    pe.wait_ge(s_wp, 8 * 16)
                pe.wait_ge(s_hT, a + 1)
                if old(0, a if not isinstance(a, int) else a - 1):
                    pe.wait_ge(s_qks, a)
                project(bQK[:, 0:NQK], hT0[:, :], hT1[:, :], Wp0[:, 0:NQK], Wp1[:, 0:NQK]).then_inc(s_qk, 1)
                project(bA[:, 0:NVB], hT0[:, :], hT1[:, :], Wp0[:, NQK:], Wp1[:, NQK:]).then_inc(s_vb, 1)

            def Fa_o(f):
                pe.wait_ge(s_otok, f + 1)
                if old(0, f if not isinstance(f, int) else f - 1):
                    pe.wait_ge(s_nmx, f)
                    pe.wait_ge(s_pr, f)
                turn(bFa, otok).then_inc(s_ocp, 1)

            def Fa_y(f, first):
                if first:
                    pe.wait_ge(s_wo, 32)
                pe.wait_ge(s_oc, f + 1)
                project(bFa[:, 0:C], oc0[:, :], oc1[:, :], Wo0[:, :], Wo1[:, :]).then_inc(s_y, 1)

            def Fa_h(f):
                pe.wait_ge(s_h2, f + 1)
                turn(bFa, h2).then_inc(s_h2Tp, 1)

            def Fa_logits(f, fp, first):
                if first:
                    pe.wait_ge(s_wr, 80)
                pe.wait_ge(s_h2T, f + 1)
                project(bFa[:, 0:E + 1], h2T0[:, fp], h2T1[:, fp], Wr0[:, :], Wr1[:, :]).then_inc(s_lg, 1)

            def Fb_up(f, fp, n, first):
                if first and n == 0:
                    pe.wait_ge(s_wu, 8 * 16)
                if n >= 2 or not isinstance(f, int) or f >= 1:
                    pe.wait_ge(s_ug, f * UN + (n - 1))
                project(bUp[n % 2][:, 0:2 * H], h2T0[:, fp], h2T1[:, fp], Wu0[:, n], Wu1[:, n]).then_inc(s_up, 1)

            def Fb_turn(f, g):
                lo, hi = GRP[g]
                pe.wait_ge(s_hid, f * UN + -(-hi * P // H))
                if g >= 2:
                    pe.wait_ge(s_htc, f * NG + (g - 1))
                elif g == 0 and (not isinstance(f, int) or f >= 1):
                    pe.wait_ge(s_htc, f * NG)
                for k in range(lo, hi):
                    last = tr(bHt[turn_bank(g)][:, (k - lo) * P:(k - lo + 1) * P], hid[:, k * P:(k + 1) * P], ident[:, :])
                last.then_inc(s_ht, 1)

            def Fb_down(f, fp, g, first):
                lo, hi = GRP[g]
                if first and g == 0:
                    pe.wait_ge(s_wd, 32)
                pe.wait_ge(s_htc, f * NG + (g + 1))
                if g == 0 and (not isinstance(f, int) or f >= 1):
                    pe.wait_ge(s_outc, f)
                for k in range(lo, hi):
                    last = mm(bDn[:, 0:C], hidT[:, turn_bank(g), k - lo, :], Wd[:, k, :], start=(k == 0), stop=(k == KT - 1))
                last.then_inc(s_dg, 1)

            def Fc_out(f):
                pe.wait_ge(s_res, f + 1)
                turn(bDn, res).then_inc(s_outp, 1)

            def step(c, par, on):
                A, Fa, Fb = on.get("A"), on.get("Fa"), on.get("Fb")
                first = isinstance(c, int)
                if "Fc" in on:
                    Fc_out(on["Fc"])
                if A is not None:
                    A_x(A)
                def up(*ns):
                    if Fb is not None:
                        for n in ns:
                            Fb_up(Fb, par, n, first and Fb == 0)
                def ht(g):
                    if Fb is not None:
                        Fb_turn(Fb, g)
                def dn(g):
                    if Fb is not None:
                        Fb_down(Fb, par, g, first and Fb == 0)
                up(0, 1, 2)
                if A is not None:
                    A_h(A)
                up(3)
                if A is not None:
                    A_proj(A)
                up(4)
                ht(0)
                up(5)
                dn(0)
                if Fa is not None:
                    Fa_o(Fa)
                up(6)
                ht(1)
                if Fa is not None:
                    Fa_y(Fa, first and Fa == 0)
                up(7)
                dn(1)
                if Fa is not None:
                    Fa_h(Fa)
                ht(2)
                up(8)
                dn(2)
                if Fa is not None:
                    Fa_logits(Fa, 1 - par, first and Fa == 0)
                up(9, 10)
                ht(3)
                up(11)
                dn(3)
                ht(4)
                dn(4)

            def prologue():
                pe.wait_ge(s_id, 2)
                for a in range(2):
                    A_x(a)
                    A_h(a)
                    A_proj(a, a == 0)

            chunks(pe, prologue, step)

        @block.scalar
        def _(act):
            f = nc.scalar.activation
            n = [0]

            def chained(ins):
                n[0] += 1
                ins.then_inc(s_act, 1)
                act.wait_ge(s_act, n[0])

            def A_xs(a):
                if old(0, a if not isinstance(a, int) else a - 1):
                    act.wait_ge(s_xT, a)
                at = a * T
                f(xs0[:, :, :], xT0[:, :, bass.ds(at, T)], ACT.Copy)
                f(xs1, xT1[:, :, bass.ds(at, T)], ACT.Copy).then_inc(s_xs, 1)

            def A_h(a):
                act.wait_ge(s_nm1, a + 1)
                f(h[:, :], bA[:, 0:C], ACT.Identity, scale=rstd1[:, 0:1], bias=nmr1[:, 0:1]).then_inc(s_h, 1)

            def A_hT(a):
                act.wait_ge(s_hTp, a + 1)
                f(hT0[:, :], bA[:, 0:P], ACT.Copy)
                f(hT1[:, :], bA[0:C1, P:2 * P], ACT.Copy).then_inc(s_hT, 1)

            def A_silu(a):
                act.wait_ge(s_qk, a + 1)
                if old(0, a if not isinstance(a, int) else a - 1):
                    act.wait_ge(s_kn, a)
                    act.wait_ge(s_qn, a)
                    act.wait_ge(s_ss, a)
                f(qk[:, 0], bQK[:, 0:C].rearrange("p (h x d) -> p x h d", h=HP, x=HX), ACT.Silu)
                f(qk[:, 1], bQK[:, C:2 * C].rearrange("p (h x d) -> p x h d", h=HP, x=HX), ACT.Silu).then_inc(s_qks, 1)
                act.wait_ge(s_vb, a + 1)
                act.wait_ge(s_z, a + 1)
                if old(0, a if not isinstance(a, int) else a - 1):
                    act.wait_ge(s_vn, a)
                f(v[:, :, :, :].rearrange("p h x d -> p (h x d)"), bA[:, 0:C], ACT.Silu).then_inc(s_vs, 1)
                act.wait_ge(s_qks, a + 1)
                f(sq[:, :, :, :, :].rearrange("p t x h d -> p (t x h d)"), qk[:, :, :, :, :].rearrange("p t x h d -> p (t x h d)"),
                  ACT.Square).then_inc(s_sq, 1)

            def A_inv(a):
                act.wait_ge(s_z, a + 1)
                chained(f(ez[:, :], zc[:, :], ACT.Exp, scale=-1.0))
                act.wait_ge(s_ss, a + 1)
                if old(0, a if not isinstance(a, int) else a - 1):
                    act.wait_ge(s_inv, a)
                f(lns[:, 24:36], ez[:, :], ACT.Ln, bias=one[:, 0:1])
                chained(f(lns[:, 0:24], ss[:, :], ACT.Ln, bias=eps6[:, 0:1]))
                if old(0, a if not isinstance(a, int) else a - 1):
                    act.wait_ge(s_kn, a)
                    act.wait_ge(s_qn, a)
                    act.wait_ge(s_vn, a)
                f(inv[:, :], lns[:, :], ACT.Exp, scale=-0.5).then_inc(s_inv, 1)

            def place(a, par, half):
                if half == 0:
                    act.wait_ge(s_vT, a + 1)
                if old(0, a if not isinstance(a, int) else a - 1):
                    act.wait_ge(s_state, a * 2 - 1 + half)
                lo = half * (T // 2)
                f(Pr[:, :, lo:lo + T // 2, :, D], vT[:, par, :, :, lo:lo + T // 2].rearrange("p h b i -> p b i h"),
                  ACT.Copy, scale=-1.0).then_inc(s_place, 1)

            def Fa_oc(q):
                act.wait_ge(s_ocp, q + 1)
                f(oc0[:, :], bFa[:, 0:P], ACT.Copy)
                f(oc1[:, :], bFa[0:C1, P:2 * P], ACT.Copy).then_inc(s_oc, 1)

            def Fa_h(q):
                act.wait_ge(s_nm2, q + 1)
                if old(0, q if not isinstance(q, int) else q - 1):
                    act.wait_ge(s_h2Tp, q)
                f(h2[:, :], xh[:, bass.ds(q, 1), :].rearrange("p z c -> p (z c)"), ACT.Identity, scale=rstd2[:, 0:1],
                  bias=nmr2[:, 0:1]).then_inc(s_h2, 1)

            def Fa_hT(q, fp):
                act.wait_ge(s_h2Tp, q + 1)
                if old(0, q if not isinstance(q, int) else q - 2):
                    act.wait_ge(s_up, q * UN - UN)
                f(h2T0[:, fp], bFa[:, 0:P], ACT.Copy)
                f(h2T1[:, fp], bFa[0:C1, P:2 * P], ACT.Copy).then_inc(s_h2T, 1)

            def Fa_exp(q):
                act.wait_ge(s_nmx, q + 1)
                if old(0, q if not isinstance(q, int) else q - 1):
                    act.wait_ge(s_gate, q)
                f(prob[:, 0:E], bFa[:, 0:E], ACT.Exp, bias=negmax[:, 0:1])
                f(prob[:, E:E + 1], bFa[:, E:E + 1], ACT.Exp, scale=-1.0, bias=neg_sgb[:, 0:1]).then_inc(s_pr, 1)

            def unit(q, fp, m):
                act.wait_ge(s_up, q * UN + (m + 1))
                if m >= RING or not isinstance(q, int) or q >= 1:
                    act.wait_ge(s_hid, q * UN + (m + 1 - RING))
                if m == 0:
                    act.wait_ge(s_gate, q + 1)
                f(sg[:, m % RING], bUp[m % 2][:, 0:H], ACT.Silu)
                f(ug[:, m % RING], bUp[m % 2][:, H:2 * H], ACT.Copy, scale=gate[:, fp, m:m + 1]).then_inc(s_ug, 1)

            def hidden(q, g):
                lo, hi = GRP[g]
                act.wait_ge(s_ht, q * NG + (g + 1))
                if g >= 2:
                    act.wait_ge(s_dg, q * NG + (g - 1))
                elif g == 0 and (not isinstance(q, int) or q >= 1):
                    act.wait_ge(s_dg, q * NG)
                w = (hi - lo) * P
                f(hidT[:, turn_bank(g)].rearrange("p k t -> p (k t)")[:, 0:w], bHt[turn_bank(g)][:, 0:w], ACT.Copy).then_inc(s_htc, 1)

            def Fc_out(q):
                act.wait_ge(s_outp, q + 1)
                at = q * T
                f(xT0[:, :, bass.ds(at, T)], bDn[:, 0:P].rearrange("c (b t) -> c b t", b=NB), ACT.Copy)
                f(xT1[:, :, bass.ds(at, T)], bDn[0:C1, P:2 * P].rearrange("c (b t) -> c b t", b=NB), ACT.Copy).then_inc(s_outc, 1)

            def step(c, par, on):
                A, Fa, Fb = on.get("A"), on.get("Fa"), on.get("Fb")
                if n[0]:
                    act.sem_clear(s_act)
                    n[0] = 0
                def units(*ms):
                    if Fb is not None:
                        for m in ms:
                            unit(Fb, par, m)
                def hT(g):
                    if Fb is not None:
                        hidden(Fb, g)
                if "R" in on:
                    place(on["R"], par, 1)
                if A is not None:
                    A_xs(A)
                if "Fc" in on:
                    Fc_out(on["Fc"])
                units(0, 1)
                if A is not None:
                    A_h(A)
                units(2)
                if A is not None:
                    A_hT(A)
                units(3)
                if A is not None:
                    A_silu(A)
                units(4)
                hT(0)
                units(5)
                if Fa is not None:
                    Fa_oc(Fa)
                units(6)
                hT(1)
                if Fa is not None:
                    Fa_h(Fa)
                if "A2" in on:
                    place(on["A2"], 1 - par, 0)
                units(7)
                if Fa is not None:
                    Fa_hT(Fa, 1 - par)
                hT(2)
                units(8)
                if A is not None:
                    A_inv(A)
                if Fa is not None:
                    Fa_exp(Fa)
                units(9, 10)
                hT(3)
                units(11)
                hT(4)

            def prologue():
                act.wait_ge(s_x, 32)
                act.wait_ge(s_const, 4)
                for a in range(2):
                    A_xs(a)
                    A_h(a)
                    A_hT(a)
                    A_silu(a)
                    A_inv(a)
                place(0, 0, 0)
                act.wait_ge(s_sgb, 1)

            chunks(act, prologue, step)

        @block.gpsimd
        def _(pool):
            tt = nc.gpsimd.tensor_tensor
            n = [0]

            def chained(ins):
                n[0] += 1
                ins.then_inc(s_pool, 1)
                pool.wait_ge(s_pool, n[0])

            def rstd(ready, a, mv, ve, out_, eps, done, used):
                pool.wait_ge(ready, a + 1)
                if old(0, a if not isinstance(a, int) else a - 1):
                    pool.wait_ge(used, a)
                chained(tt(ve[:, :], mv[:, 1:2], eps[:, :], ALU.add))
                tt(out_[:, :], ve[:, :], neg_half[:, :], ALU.pow).then_inc(done, 1)

            def A_norm(a):
                pool.wait_ge(s_inv, a + 1)
                if old(0, a if not isinstance(a, int) else a - 1):
                    pool.wait_ge(s_scr, a * 128)
                    pool.wait_ge(s_vT, a)
                tt(kqn[:, 1].rearrange("p x (h d) -> p (x h) d", d=D), qk[:, 0].rearrange("p x h d -> p (x h) d"),
                   inv[:, 0:12].unsqueeze(2).to_broadcast([P, NH, D]), ALU.mult).then_inc(s_qn, 1)
                pool.wait_ge(s_vs, a + 1)
                tt(vn[:, :, :, :].rearrange("p h x d -> p (h x) d"), v[:, :, :, :].rearrange("p h x d -> p (h x) d"),
                   inv[:, 24:36].unsqueeze(2).to_broadcast([P, NH, D]), ALU.mult).then_inc(s_vn, 1)

            def out_half(c, par, half):
                pool.wait_ge(s_state, c * 2 + (half + 1))
                if half == 0:
                    pool.wait_ge(s_QB[par], loads(c, par))
                lo = half * (T // 2)
                tt(PQ[:, :, :].rearrange("p (i b h) d -> p i b (h d)", i=T // 2, b=BR),
                   SH[:, par, lo:lo + T // 2].rearrange("p i b h d -> p i b (h d)"),
                   QB[:, par, :, lo:lo + T // 2].rearrange("p b i h d -> p i b (h d)"), ALU.mult).then_inc(s_pq, 1)
                pool.wait_ge(s_pq, c * 2 + (half + 1))
                for w in (8, 4, 2):
                    chained(tt(PQ[:, :, 0:w], PQ[:, :, 0:w], PQ[:, :, w:2 * w], ALU.add))
                if half == 0 and old(0, c if not isinstance(c, int) else c - 1):
                    pool.wait_ge(s_otok, c)
                s = PQ[:, :, 0:2].rearrange("p (i b h) d -> p i b h d", i=T // 2, b=BR)
                tt(oT[:, :, :, lo:lo + T // 2].rearrange("p h b i -> p i b h"), s[:, :, :, :, 0], s[:, :, :, :, 1],
                   ALU.add).then_inc(s_oT, 1)

            def hidden(q, m):
                pool.wait_ge(s_ug, q * UN + (m + 1))
                if m == 0 and (not isinstance(q, int) or q >= 1):
                    pool.wait_ge(s_ht, q * NG)
                tt(hid[:, m * H:(m + 1) * H], sg[:, m % RING], ug[:, m % RING], ALU.mult).then_inc(s_hid, 1)

            def step(c, par, on):
                A, Fa, Fb, R = on.get("A"), on.get("Fa"), on.get("Fb"), on.get("R")
                if n[0]:
                    pool.sem_clear(s_pool)
                    n[0] = 0
                def units(*ms):
                    if Fb is not None:
                        for m in ms:
                            hidden(Fb, m)
                if A is not None:
                    rstd(s_st1, A, mv1, ve1, rstd1, eps6, s_rs1, s_h)
                if Fa is not None:
                    out_half(Fa, 1 - par, 1)
                units(0, 1, 2, 3, 4, 5)
                if Fa is not None:
                    rstd(s_st2, Fa, mv2, ve2, rstd2, eps5, s_rs2, s_h2)
                units(6, 7)
                if R is not None:
                    out_half(R, par, 0)
                if A is not None:
                    A_norm(A)
                units(8, 9, 10, 11)

            def prologue():
                pool.memset(ident[:, :], 0.0).then_inc(s_id, 1)
                pool.wait_ge(s_id, 1)
                pool.affine_select(out=ident[:, :], in_=ident[:, :], compare_op=ALU.not_equal, fill=1.0, base=0,
                                   pattern=[[-1, P]], channel_multiplier=1).then_inc(s_id, 1)
                for t, val in ((neg_half, -0.5), (eps6, 1e-6), (eps5, 1e-5), (one, 1.0)):
                    pool.memset(t[:, :], val).then_inc(s_const, 1)
                pool.memset(lower[:, :, :], 1.0).then_inc(s_low, 1)
                pool.wait_ge(s_low, 1)
                pool.affine_select(out=lower[:, :, :], in_=lower[:, :, :], compare_op=ALU.is_gt, fill=0.0, base=0,
                                   pattern=[[1, E], [-1, E]], channel_multiplier=0).then_inc(s_low, 1)
                pool.memset(SH[:, 1, T - 1], 0.0).then_inc(s_zero, 1)
                pool.wait_ge(s_const, 4)
                for a in range(2):
                    rstd(s_st1, a, mv1, ve1, rstd1, eps6, s_rs1, s_h)
                    A_norm(a)

            chunks(pool, prologue, step)

        @block.vector
        def _(dve):
            tt, ts = nc.vector.tensor_tensor, nc.vector.tensor_scalar
            n = [0]

            def count(ins):
                n[0] += 1
                ins.then_inc(s_chain, 1)
                return s_chain, n[0]

            def stats(src, st, mv, done):
                dve.wait_ge(*count(nc.vector.bn_stats(st[:, :], src)))
                nc.vector.bn_aggr(mv[:, :], st[:, :]).then_inc(done, 1)

            def A_stats(a):
                dve.wait_ge(s_xT, a + 1)
                if old(0, a if not isinstance(a, int) else a - 1):
                    dve.wait_ge(s_rs1, a)
                    dve.wait_ge(s_nm1, a)
                stats(bA[:, 0:C], st1, mv1, s_st1)

            def nmr(a, mv, rs, out_, rs_ready, used, done):
                dve.wait_ge(rs_ready, a + 1)
                if old(0, a if not isinstance(a, int) else a - 1):
                    dve.wait_ge(used, a)
                nc.vector.scalar_tensor_tensor(out=out_[:, :], in0=mv[:, 0:1], scalar=-1.0, in1=rs[:, :], op0=ALU.mult,
                                               op1=ALU.mult).then_inc(done, 1)

            def A_xh(a):
                dve.wait_ge(s_h, a + 1)
                tt(xh[:, bass.ds(a, 1), :].rearrange("p z c -> p (z c)"), bA[:, 0:C], h[:, :], ALU.add).then_inc(s_xh, 1)

            def A_z(a):
                dve.wait_ge(s_vb, a + 1)
                if old(0, a if not isinstance(a, int) else a - 1):
                    dve.wait_ge(s_inv, a)
                ts(zc[:, :], bA[:, C:C + NH], -40.0, None, ALU.max).then_inc(s_z, 1)

            def A_ss(a):
                dve.wait_ge(s_sq, a + 1)
                if old(0, a if not isinstance(a, int) else a - 1):
                    dve.wait_ge(s_inv, a)
                nc.vector.tensor_reduce(ss[:, :], sq[:, :, :, :, :].rearrange("p t x h d -> p (t x h) d"), X, ALU.add).then_inc(s_ss, 1)

            def A_kn(a):
                dve.wait_ge(s_inv, a + 1)
                if old(0, a if not isinstance(a, int) else a - 1):
                    dve.wait_ge(s_scr, a * 128)
                w = count(tt(ksc[:, :, :], inv[:, 12:24].rearrange("p (x h) -> p x h", x=HX),
                             inv[:, 24:36].rearrange("p (h x) -> p x h", x=HX), ALU.mult))
                dve.wait_ge(*w)
                tt(kqn[:, 0].rearrange("p x (h d) -> p (x h) d", d=D), qk[:, 1].rearrange("p x h d -> p (x h) d"),
                   ksc[:, :, :].rearrange("p x h -> p (x h)").unsqueeze(2).to_broadcast([P, NH, D]), ALU.mult).then_inc(s_kn, 1)

            def A_vT(a, par):
                dve.wait_ge(s_vn, a + 1)
                if old(0, a if not isinstance(a, int) else a - 2):
                    dve.wait_ge(s_place, a * 2 - 2)
                nc.vector.transpose(vT[:, par].rearrange("p h b i -> p (h b i)"), vn[:, :, :, :].rearrange("p h x d -> p (h x d)")).then_inc(s_vT, 1)

            def Fa_otok(q):
                dve.wait_ge(s_oT, q * 2 + 2)
                if old(0, q if not isinstance(q, int) else q - 1):
                    dve.wait_ge(s_ocp, q)
                nc.vector.transpose(otok[:, :], oT[:, :, :, :].rearrange("p h b i -> p (h b i)")).then_inc(s_otok, 1)

            def Fa_x1(q):
                dve.wait_ge(s_y, q + 1)
                if old(0, q if not isinstance(q, int) else q - 1):
                    dve.wait_ge(s_rs2, q)
                    dve.wait_ge(s_nm2, q)
                xq = xh[:, bass.ds(q, 1), :].rearrange("p z c -> p (z c)")
                dve.wait_ge(*count(tt(xq, bFa[:, 0:C], xq, ALU.add)))
                stats(xq, st2, mv2, s_st2)

            def Fa_max(q):
                dve.wait_ge(s_lg, q + 1)
                nc.vector.tensor_reduce(negmax[:, :], bFa[:, 0:E], X, ALU.max, negate=True).then_inc(s_nmx, 1)

            def Fa_gates(q, fp):
                pe_, po = prob[:, 0:E].unsqueeze(2).to_broadcast([P, E, E]), prob[:, 0:E].unsqueeze(1).to_broadcast([P, E, E])
                w = {}
                def rank1():
                    dve.wait_ge(s_pr, q + 1)
                    if old(0, q if not isinstance(q, int) else q - 2):
                        dve.wait_ge(s_ug, q * UN - UN)
                    count(tt(gt[:, :, :], po, pe_, ALU.is_gt))
                    w["eq"] = count(tt(eq[:, :, :], po, pe_, ALU.is_equal))
                    count(ts(den[:, 1:2], prob[:, E:E + 1], 1.0, None, ALU.add))
                def rank2():
                    dve.wait_ge(*w["eq"])
                    w["eq"] = count(tt(eq[:, :, :], eq[:, :, :], lower[:, :, :], ALU.mult))
                def rank3():
                    dve.wait_ge(*w["eq"])
                    w["gt"] = count(tt(gt[:, :, :], gt[:, :, :], eq[:, :, :], ALU.add))
                def rank4():
                    dve.wait_ge(*w["gt"])
                    w["rank"] = count(nc.vector.tensor_reduce(rank[:, :], gt[:, :, :], X, ALU.add))
                def pick():
                    dve.wait_ge(*w["rank"])
                    w["sel"] = count(nc.vector.scalar_tensor_tensor(out=sel[:, :], in0=rank[:, :], scalar=2.0, in1=prob[:, 0:E],
                                                                    op0=ALU.is_lt, op1=ALU.mult))
                def total():
                    dve.wait_ge(*w["sel"])
                    w["den"] = count(nc.vector.tensor_reduce(den[:, 0:1], sel[:, :], X, ALU.add))
                def recip():
                    dve.wait_ge(*w["den"])
                    w["rden"] = count(nc.vector.reciprocal(rden[:, :], den[:, :]))
                def coefs():
                    dve.wait_ge(*w["rden"])
                    w["om"] = count(ts(coef[:, :], rden[:, 1:2], -1.0, 1.0, ALU.mult, ALU.add))
                    count(ts(gate[:, fp, E:UN], one[:, 0:1].to_broadcast([P, UN - E]), rden[:, 1:2], None, ALU.mult))
                def coef2():
                    dve.wait_ge(*w["om"])
                    w["co"] = count(tt(coef[:, :], coef[:, :], rden[:, 0:1], ALU.mult))
                def last():
                    dve.wait_ge(*w["co"])
                    ts(gate[:, fp, 0:E], sel[:, :], coef[:, 0:1], None, ALU.mult).then_inc(s_gate, 1)
                return [rank1, rank2, rank3, rank4, pick, total, recip, coefs, coef2, last]

            def Fc_res(q):
                dve.wait_ge(s_dg, q * NG + NG)
                if old(0, q if not isinstance(q, int) else q - 1):
                    dve.wait_ge(s_outp, q)
                xq = xh[:, bass.ds(q, 1), :].rearrange("p z c -> p (z c)")
                tt(res[:, :], bDn[:, 0:C], xq, ALU.add).then_inc(s_res, 1)

            def step(c, par, on):
                A, A2, R, Fa, Fc = (on.get(k) for k in ("A", "A2", "R", "Fa", "Fc"))
                work = []
                if Fc is not None:
                    work += [(1, lambda: Fc_res(Fc))]
                if A2 is not None:
                    work += [(3, lambda: A_vT(A2, 1 - par))]
                if A is not None:
                    work += [(4, lambda: A_stats(A)),
                             (10, lambda: nmr(A, mv1, rstd1, nmr1, s_rs1, s_h, s_nm1)), (16, lambda: A_xh(A)),
                             (23, lambda: A_z(A)), (29, lambda: A_ss(A)), (58, lambda: A_kn(A))]
                if Fa is not None:
                    work += [(24, lambda: Fa_otok(Fa)), (31, lambda: Fa_x1(Fa)),
                             (36, lambda: nmr(Fa, mv2, rstd2, nmr2, s_rs2, s_h2, s_nm2)), (44, lambda: Fa_max(Fa))]
                    work += [(50 + i, g) for i, g in enumerate(Fa_gates(Fa, 1 - par))]
                work.sort(key=lambda w: w[0])

                def fill(slot):
                    while work and work[0][0] <= slot:
                        work.pop(0)[1]()

                if R is not None:
                    dve.wait_ge(s_KB[par], loads(c, par))
                    Sb = [None, None]
                    for i in range(T):
                        prev = SH[:, 1 - par, T - 1] if i == 0 else SH[:, par, i - 1]
                        slot = 4 * i
                        if i % (T // 2) == 0:
                            dve.wait_ge(s_place, c * 2 + (i // (T // 2) + 1))
                            if not isinstance(c, int) or c >= 2:
                                dve.wait_ge(s_pq, c * 2 - 3 + i // (T // 2))
                        def each(fn, waits):
                            got = []
                            for br in range(BR):
                                if waits[br] is not None:
                                    dve.wait_ge(*waits[br])
                                got.append(fn(br))
                            return got
                        w = each(lambda br: count(tt(Pr[:, br, i, :, 0:D], prev[:, br], KB[:, par, br, i], ALU.mult)), Sb)
                        fill(slot)
                        w = each(lambda br: count(nc.vector.tensor_reduce(u[:, i % 2, br], Pr[:, br, i], X, ALU.add, negate=True)), w)
                        fill(slot + 1)
                        w = each(lambda br: count(tt(TT[:, i % 2, br], KB[:, par, br, i],
                                                     u[:, i % 2, br].unsqueeze(2).to_broadcast([P, HP, D]), ALU.mult)), w)
                        fill(slot + 2)
                        def grow(br):
                            ins = tt(SH[:, par, i, br], prev[:, br], TT[:, i % 2, br], ALU.add)
                            if i % (T // 2) == T // 2 - 1 and br == BR - 1:
                                ins.then_inc(s_state, 1)
                                return s_state, c * 2 + (i // (T // 2) + 1)
                            return count(ins)
                        Sb = each(grow, w)
                        fill(slot + 3)
                fill(1000)
                dve.wait_ge(s_chain, n[0]) if n[0] else None
                if R is not None:
                    dve.wait_ge(s_state, c * 2 + 2)
                if n[0]:
                    dve.sem_clear(s_chain)
                n[0] = 0

            def prologue():
                dve.wait_ge(s_const, 4)
                dve.wait_ge(s_low, 2)
                dve.wait_ge(s_zero, 1)
                for a in range(2):
                    A_stats(a)
                    nmr(a, mv1, rstd1, nmr1, s_rs1, s_h, s_nm1)
                    A_xh(a)
                    A_z(a)
                    A_ss(a)
                    A_kn(a)
                    if a == 0:
                        A_vT(0, 0)
                dve.wait_ge(s_wr, 80)
                ts(neg_sgb[:, :], sgb[:, :], -1.0, None, ALU.mult).then_inc(s_sgb, 1)
                dve.wait_ge(s_chain, n[0])
                dve.sem_clear(s_chain)
                n[0] = 0

            chunks(dve, prologue, step)


_INS = ['x', 'L0_conv_Wq', 'L0_conv_Wk', 'L0_conv_Wv', 'L0_conv_Wb', 'L0_conv_Wo', 'L0_ffn_router_w', 'L0_ffn_w_gate',
        'L0_ffn_w_up', 'L0_ffn_w_down', 'L0_ffn_ws_gate', 'L0_ffn_ws_up', 'L0_ffn_ws_down', 'L0_ffn_sg_w', 'L0_ffn_sg_b']


def kernel(**inputs):
    import numpy as _np
    import concourse.bacc as _bacc
    from concourse import mybir as _mybir
    from concourse.bass_utils import run_bass_kernel_spmd as _run

    nc = _bacc.Bacc("TRN2", target_bir_lowering=False, num_devices=1)
    arrays, args = {}, []
    for name in _INS:
        a = _np.ascontiguousarray(inputs[name])
        shape = (NB, C, L) if name == 'x' else a.shape
        a = a.reshape(shape)
        arrays[f"in_{name}_dram"] = a
        args.append(nc.dram_tensor(f"in_{name}_dram", a.shape, _mybir.dt.from_np(a.dtype), kind="ExternalInput").ap())
    o = nc.dram_tensor("out_0_dram", (NB, C, L), _mybir.dt.float32, kind="ExternalOutput").ap()
    build(nc, *args, o)
    r = _run(nc, [arrays], core_ids=[0])
    return r.results[0]["out_0_dram"].reshape(NB, C, 16, 16)
```

```python
import concourse.bass as bass
from concourse import mybir
from contextlib import ExitStack

F32 = mybir.dt.float32
ALU = mybir.AluOpType
ACT = mybir.ActivationFunctionType
X = mybir.AxisListType.X

NB, C, L = 8, 192, 256
NH, D = 12, 16
T = 16
NC = L // T
P = 128
C0, C1 = P, C - P
BP, BR, HP, HX = 4, 2, 6, 2
G = HP * D
E, H, HS = 8, 192, 768
UN = E + HS // H
HID = UN * H
KT = HID // P
GRP = [(0, 4), (4, 8), (8, 12), (12, 16), (16, 18)]
NG = len(GRP)
RING = 4
NQK, NVB = 2 * C, C + NH
LN_EXP = "natural_log_exp_and_others"


def build(nc, x, Wq, Wk, Wv, Wb, Wo, router_w, w_gate, w_up, w_down, ws_gate, ws_up, ws_down, sg_w, sg_b, out):
    ctx = ExitStack()
    with ctx:
        def sb(name, shape):
            return ctx.enter_context(nc.sbuf_tensor(name, shape, F32))

        def sem(name):
            return ctx.enter_context(nc.semaphore(name))

        kq_dram = nc.dram_tensor("kq_scratch", [NC, 2, BP, HX, BR * T, G], F32, kind="Internal").ap()

        xT0 = sb("xT0", [C0, NB, L])
        low = sb("low", [P, UN * 2 * H])
        xT1 = low[C1:P, 0:NB * L].rearrange("c (b l) -> c b l", b=NB)
        ident = sb("ident", [P, P])
        Wp0, Wp1 = sb("Wp0", [C0, NQK + NVB]), sb("Wp1", [C1, NQK + NVB])
        Wo0, Wo1 = sb("Wo0", [C0, C]), sb("Wo1", [C1, C])
        Wr0, Wr1 = sb("Wr0", [C0, E + 1]), sb("Wr1", [C1, E + 1])
        Wu0 = sb("Wu0", [C0, UN, 2 * H])
        Wu1 = low[0:C1, :].rearrange("c (n h) -> c n h", n=UN)
        Wd = sb("Wd", [P, KT, C])
        xh = sb("xh", [P, NC, C])
        neg_half, eps6, eps5, one = sb("neg_half", [P, 1]), sb("eps6", [P, 1]), sb("eps5", [P, 1]), sb("one", [P, 1])
        sgb, neg_sgb = sb("sgb", [P, 1]), sb("neg_sgb", [P, 1])
        lower = sb("lower", [P, E, E])
        xs0, xs = sb("xs0", [C0, NB, T]), sb("xs1", [P, NB, T])
        xs1 = xs[C1:P]
        st1, mv1 = sb("st1", [P, 6]), sb("mv1", [P, 2])
        ve1, rstd1, nmr1 = sb("ve1", [P, 1]), sb("rstd1", [P, 1]), sb("nmr1", [P, 1])
        h = sb("h", [P, C])
        hT0, hT1 = sb("hT0", [C0, P]), sb("hT1", [C1, P])
        zc = sb("zc", [P, NH])
        qk = sb("qk", [P, 2, HX, HP, D])
        sq = sb("sq", [P, 2, HX, HP, D])
        v = sb("v", [P, HP, HX, D])
        ss, ez, lns, inv = sb("ss", [P, 24]), sb("ez", [P, NH]), sb("lns", [P, 36]), sb("inv", [P, 36])
        ksc = sb("ksc", [P, HX, HP])
        kqn = sb("kqn", [P, 2, HX, G])
        vn = sb("vn", [P, HP, HX, D])
        vT = sb("vT", [P, 2, HP, BR, T])
        KB = sb("KB", [P, 2, BR, T, HP, D])
        QB = sb("QB", [P, 2, BR, T, HP, D])
        Pr = sb("Pr", [P, BR, T, HP, D + 1])
        u = sb("u", [P, 2, BR, HP])
        TT = sb("TT", [P, 2, BR, HP, D])
        SH = sb("SH", [P, 2, T, BR, HP, D])
        PQ = sb("PQ", [P, T // 2 * BR * HP, D])
        oT = sb("oT", [P, HP, BR, T])
        otok = sb("otok", [P, C])
        oc0, oc1 = sb("oc0", [C0, P]), sb("oc1", [C1, P])
        st2, mv2 = sb("st2", [P, 6]), sb("mv2", [P, 2])
        ve2, rstd2, nmr2 = sb("ve2", [P, 1]), sb("rstd2", [P, 1]), sb("nmr2", [P, 1])
        h2 = sb("h2", [P, C])
        h2T0, h2T1 = sb("h2T0", [C0, 2, P]), sb("h2T1", [C1, 2, P])
        negmax, prob = sb("negmax", [P, 1]), sb("prob", [P, E + 1])
        gt, eq, rank = sb("gt", [P, E, E]), sb("eq", [P, E, E]), sb("rank", [P, E])
        sel, den, rden, coef = sb("sel", [P, E]), sb("den", [P, 2]), sb("rden", [P, 2]), sb("coef", [P, 1])
        gate = sb("gate", [P, 2, UN])
        sg, ug = sb("sg", [P, RING, H]), sb("ug", [P, RING, H])
        hid = sb("hid", [P, HID])
        hidT = sb("hidT", [P, 2, 4, P])
        res = sb("res", [P, C])

        bank = [ctx.enter_context(nc.psum_tensor(f"bank{i}", [P, 512], F32)) for i in range(8)]
        bA, bQK, bFa, bDn = bank[0], bank[1], bank[2], bank[3]
        bUp, bHt = bank[4:6], bank[6:8]

        s_x, s_wp, s_wo, s_wr, s_wu, s_wd = (sem(n) for n in ("x_in", "wp_in", "wo_in", "wr_in", "wu_in", "wd_in"))
        s_const, s_zero, s_id, s_low = sem("consts_ready"), sem("state_zero"), sem("ident_ready"), sem("lower_ready")
        s_sgb = sem("sgb_ready")
        s_chain = sem("dve_chain")
        s_pool = sem("pool_chain")
        s_act = sem("act_chain")
        s_xs, s_xT, s_st1, s_rs1, s_nm1, s_h, s_xh = (sem(n) for n in (
            "xs_ready", "xT_ready", "stats1_ready", "rstd1_ready", "nmr1_ready", "h_ready", "xh_ready"))
        s_hTp, s_hT, s_qk, s_vb, s_z, s_qks, s_vs, s_sq, s_ss, s_inv = (sem(n) for n in (
            "hT_psum_ready", "hT_ready", "qk_ready", "vb_ready", "z_ready", "qk_silu_ready", "v_silu_ready",
            "squares_ready", "norms_ready", "inv_ready"))
        s_kn, s_qn, s_vn, s_vT, s_place = (sem(n) for n in (
            "k_normed", "q_normed", "v_normed", "vT_ready", "v_placed"))
        s_scr = sem("scratch_written")
        s_KB, s_QB = [sem("KB_in_even"), sem("KB_in_odd")], [sem("QB_in_even"), sem("QB_in_odd")]
        s_state, s_pq, s_oT = sem("states_ready"), sem("states_read"), sem("o_summed")
        s_otok, s_ocp, s_oc, s_y, s_st2, s_rs2, s_nm2, s_h2 = (sem(n) for n in (
            "o_by_token", "oc_psum_ready", "oc_ready", "y_ready", "stats2_ready", "rstd2_ready", "nmr2_ready", "h2_ready"))
        s_h2Tp, s_h2T, s_lg, s_nmx, s_pr, s_gate = (sem(n) for n in (
            "h2T_psum_ready", "h2T_ready", "logits_ready", "negmax_ready", "probs_ready", "gates_ready"))
        s_up, s_ug, s_hid = sem("up_ready"), sem("unit_copied"), sem("hidden_ready")
        s_ht, s_htc, s_dg = sem("hidT_psum_ready"), sem("hidT_ready"), sem("down_group_done")
        s_res, s_outp, s_outc, s_out = sem("res_ready"), sem("outT_psum_ready"), sem("out_copied"), sem("out_written")

        block = ctx.enter_context(nc.Block())

        def chunks(eng, step):
            def stages(c):
                return dict(X=c + 3, A=c + 2, A2=c + 1, R=c, Fa=c - 1, Fb=c - 2, Fc=c - 3)
            def edge(c):
                step(c, c % 2, {k: n for k, n in stages(c).items() if 0 <= n < NC})
            for c in range(-3, 4):
                edge(c)
            with eng.Fori(0, 4) as k:
                for j in range(2):
                    c = eng.snap(k * 2 + (4 + j))
                    step(c, j, stages(c))
            for c in range(12, NC + 3):
                edge(c)

        def loads(c, par):
            return c * 8 + (16 - 8 * par)

        def old(w, n):
            return not isinstance(n, int) or n >= 0

        def turn_bank(g):
            return g % 2

        @block.sync
        def _(sp):
            def scratch(a):
                sp.wait_ge(s_kn, a + 1)
                sp.wait_ge(s_qn, a + 1)
                for t in range(2):
                    for bp in range(BP):
                        sp.dma_start(kq_dram[bass.ds(a, 1), t, bp].rearrange("z x r g -> r (z x) g"),
                                     kqn[32 * bp:32 * bp + 32, t]).then_inc(s_scr, 16)

            def spread(a, par):
                sp.wait_ge(s_scr, (a + 1) * 128)
                if old(0, a if not isinstance(a, int) else a - 2):
                    sp.wait_ge(s_state, a * 2 - 2)
                sp.dma_start(KB[:, par].rearrange("p b i h d -> p (b i h d)"),
                             kq_dram[bass.ds(a, 1), 0].rearrange("z b x r g -> (z b x) (r g)").unsqueeze(1).to_broadcast(
                                 [BP * HX, D, BR * T * G])).then_inc(s_KB[par], 16)
                if old(0, a if not isinstance(a, int) else a - 2):
                    sp.wait_ge(s_pq, a * 2 - 2)
                sp.dma_start(QB[:, par].rearrange("p b i h d -> p (b i h d)"),
                             kq_dram[bass.ds(a, 1), 1].rearrange("z b x r g -> (z b x) (r g)").unsqueeze(1).to_broadcast(
                                 [BP * HX, D, BR * T * G])).then_inc(s_QB[par], 16)

            def load():
                sp.dma_start(xT0[:, :, :], x[:, 0:C0].rearrange("b c l -> c b l")).then_inc(s_x, 16)
                sp.dma_start(xT1[:, :, :], x[:, C0:C].rearrange("b c l -> c b l")).then_inc(s_x, 16)
                for i, w in enumerate((Wq, Wk, Wv)):
                    sp.dma_start(Wp0[:, i * C:i * C + C], w[0:C0, :]).then_inc(s_wp, 16)
                    sp.dma_start(Wp1[:, i * C:i * C + C], w[C0:C, :]).then_inc(s_wp, 16)
                sp.dma_start(Wp0[:, 3 * C:3 * C + NH], Wb[0:C0, :]).then_inc(s_wp, 16)
                sp.dma_start(Wp1[:, 3 * C:3 * C + NH], Wb[C0:C, :]).then_inc(s_wp, 16)
                sp.dma_start(Wo0[:, :], Wo[0:C0, :]).then_inc(s_wo, 16)
                sp.dma_start(Wo1[:, :], Wo[C0:C, :]).then_inc(s_wo, 16)
                sp.dma_start(Wr0[:, 0:E], router_w[0:C0, :]).then_inc(s_wr, 16)
                sp.dma_start(Wr1[:, 0:E], router_w[C0:C, :]).then_inc(s_wr, 16)
                sp.dma_start(Wr0[:, E:E + 1], sg_w[0:C0, :]).then_inc(s_wr, 16)
                sp.dma_start(Wr1[:, E:E + 1], sg_w[C0:C, :]).then_inc(s_wr, 16)
                sp.dma_start(sgb[:, :], sg_b.rearrange("(a n) -> a n", a=1).to_broadcast([P, 1])).then_inc(s_wr, 16)
                for half, we, ws in ((0, w_gate, ws_gate), (H, w_up, ws_up)):
                    for W, lo, hi in ((Wu0, 0, C0), (Wu1, C0, C)):
                        sp.dma_start(W[:, 0:E, half:half + H], we[:, lo:hi, :].rearrange("e c h -> c e h")).then_inc(s_wu, 16)
                        sp.dma_start(W[:, E:UN, half:half + H], ws[lo:hi, :].rearrange("c (s h) -> c s h", h=H)).then_inc(s_wu, 16)
                ke = E * H // P
                sp.dma_start(Wd[:, 0:ke, :], w_down.rearrange("e h c -> (e h) c").rearrange("(k p) c -> p k c", p=P)).then_inc(s_wd, 16)
                sp.dma_start(Wd[:, ke:KT, :], ws_down.rearrange("(k p) c -> p k c", p=P)).then_inc(s_wd, 16)

            def step(c, par, on):
                if "A2" in on:
                    scratch(on["A2"])
                    spread(on["A2"], 1 - par)

            load()
            chunks(sp, step)
            sp.wait_ge(s_outc, NC)
            sp.dma_start(out[:, 0:C0].rearrange("b c l -> c b l"), xT0[:, :, :]).then_inc(s_out, 16)
            sp.dma_start(out[:, C0:C].rearrange("b c l -> c b l"), xT1[:, :, :]).then_inc(s_out, 16)
            sp.wait_ge(s_out, 32)

        @block.tensor
        def _(pe):
            mm, tr = nc.tensor.matmul, nc.tensor.transpose

            def project(dst, a0, a1, w0, w1):
                mm(dst, a0, w0, start=True, stop=False)
                return mm(dst, a1, w1, start=False, stop=True)

            def turn(b, src):
                tr(b[:, 0:P], src[:, 0:C0], ident[:, :])
                return tr(b[0:C1, P:2 * P], src[:, C0:C], ident[:, :])

            def A_x(a):
                pe.wait_ge(s_xs, a + 1)
                if old(0, a if not isinstance(a, int) else a - 1):
                    pe.wait_ge(s_z, a)
                    pe.wait_ge(s_vs, a)
                tr(bA[:, 0:C0], xs0[:, :, :].rearrange("c b t -> c (b t)"), ident[:, :])
                tr(bA[:, C0:C], xs1.rearrange("c b t -> c (b t)"), ident[C1:P, C1:P]).then_inc(s_xT, 1)

            def A_h(a):
                pe.wait_ge(s_h, a + 1)
                pe.wait_ge(s_xh, a + 1)
                turn(bA, h).then_inc(s_hTp, 1)

            def A_proj(a, first=False):
                if first:
                    pe.wait_ge(s_wp, 8 * 16)
                pe.wait_ge(s_hT, a + 1)
                if old(0, a if not isinstance(a, int) else a - 1):
                    pe.wait_ge(s_qks, a)
                project(bQK[:, 0:NQK], hT0[:, :], hT1[:, :], Wp0[:, 0:NQK], Wp1[:, 0:NQK]).then_inc(s_qk, 1)
                project(bA[:, 0:NVB], hT0[:, :], hT1[:, :], Wp0[:, NQK:], Wp1[:, NQK:]).then_inc(s_vb, 1)

            def Fa_o(f):
                pe.wait_ge(s_otok, f + 1)
                if old(0, f if not isinstance(f, int) else f - 1):
                    pe.wait_ge(s_nmx, f)
                    pe.wait_ge(s_pr, f)
                turn(bFa, otok).then_inc(s_ocp, 1)

            def Fa_y(f, first):
                if first:
                    pe.wait_ge(s_wo, 32)
                pe.wait_ge(s_oc, f + 1)
                project(bFa[:, 0:C], oc0[:, :], oc1[:, :], Wo0[:, :], Wo1[:, :]).then_inc(s_y, 1)

            def Fa_h(f):
                pe.wait_ge(s_h2, f + 1)
                turn(bFa, h2).then_inc(s_h2Tp, 1)

            def Fa_logits(f, fp, first):
                if first:
                    pe.wait_ge(s_wr, 80)
                pe.wait_ge(s_h2T, f + 1)
                project(bFa[:, 0:E + 1], h2T0[:, fp], h2T1[:, fp], Wr0[:, :], Wr1[:, :]).then_inc(s_lg, 1)

            def Fb_up(f, fp, n, first):
                if first and n == 0:
                    pe.wait_ge(s_wu, 8 * 16)
                if n >= 2 or not isinstance(f, int) or f >= 1:
                    pe.wait_ge(s_ug, f * UN + (n - 1))
                project(bUp[n % 2][:, 0:2 * H], h2T0[:, fp], h2T1[:, fp], Wu0[:, n], Wu1[:, n]).then_inc(s_up, 1)

            def Fb_turn(f, g):
                lo, hi = GRP[g]
                pe.wait_ge(s_hid, f * UN + -(-hi * P // H))
                if g >= 2:
                    pe.wait_ge(s_htc, f * NG + (g - 1))
                elif g == 0 and (not isinstance(f, int) or f >= 1):
                    pe.wait_ge(s_htc, f * NG)
                for k in range(lo, hi):
                    last = tr(bHt[turn_bank(g)][:, (k - lo) * P:(k - lo + 1) * P], hid[:, k * P:(k + 1) * P], ident[:, :])
                last.then_inc(s_ht, 1)

            def Fb_down(f, fp, g, first):
                lo, hi = GRP[g]
                if first and g == 0:
                    pe.wait_ge(s_wd, 32)
                pe.wait_ge(s_htc, f * NG + (g + 1))
                if g == 0 and (not isinstance(f, int) or f >= 1):
                    pe.wait_ge(s_outc, f)
                for k in range(lo, hi):
                    last = mm(bDn[:, 0:C], hidT[:, turn_bank(g), k - lo, :], Wd[:, k, :], start=(k == 0), stop=(k == KT - 1))
                last.then_inc(s_dg, 1)

            def Fc_out(f):
                pe.wait_ge(s_res, f + 1)
                turn(bDn, res).then_inc(s_outp, 1)

            def step(c, par, on):
                X_, A, Fa, Fb, Fc = (on.get(k) for k in ("X", "A", "Fa", "Fb", "Fc"))
                first = isinstance(c, int)

                def do(n, fn, *args):
                    if n is not None:
                        fn(n, *args)

                def up(*ns):
                    for n in ns:
                        do(Fb, Fb_up, par, n, first and Fb == 0)

                def ht(g):
                    do(Fb, Fb_turn, g)

                def dn(g):
                    do(Fb, Fb_down, par, g, first and Fb == 0)

                up(0)
                do(A, A_h)
                up(1)
                do(Fc, Fc_out)
                do(A, A_proj, first and A == 0)
                up(2)
                up(3)
                do(Fa, Fa_o)
                ht(0)
                up(4)
                do(Fa, Fa_y, first and Fa == 0)
                dn(0)
                up(5)
                up(6)
                do(Fa, Fa_h)
                ht(1)
                up(7)
                do(Fa, Fa_logits, 1 - par, first and Fa == 0)
                dn(1)
                up(8)
                ht(2)
                do(X_, A_x)
                up(9)
                up(10)
                up(11)
                ht(3)
                dn(2)
                ht(4)
                dn(3)
                dn(4)

            pe.wait_ge(s_id, 2)
            chunks(pe, step)

        @block.scalar
        def _(act):
            f = nc.scalar.activation
            n = [0]

            def chained(ins):
                n[0] += 1
                ins.then_inc(s_act, 1)
                act.wait_ge(s_act, n[0])

            def A_xs(a):
                if old(0, a if not isinstance(a, int) else a - 1):
                    act.wait_ge(s_xT, a)
                at = a * T
                f(xs0[:, :, :], xT0[:, :, bass.ds(at, T)], ACT.Copy)
                f(xs1, xT1[:, :, bass.ds(at, T)], ACT.Copy).then_inc(s_xs, 1)

            def A_h(a):
                act.wait_ge(s_nm1, a + 1)
                f(h[:, :], bA[:, 0:C], ACT.Identity, scale=rstd1[:, 0:1], bias=nmr1[:, 0:1]).then_inc(s_h, 1)

            def A_hT(a):
                act.wait_ge(s_hTp, a + 1)
                f(hT0[:, :], bA[:, 0:P], ACT.Copy)
                f(hT1[:, :], bA[0:C1, P:2 * P], ACT.Copy).then_inc(s_hT, 1)

            def A_silu(a):
                act.wait_ge(s_qk, a + 1)
                if old(0, a if not isinstance(a, int) else a - 1):
                    act.wait_ge(s_kn, a)
                    act.wait_ge(s_qn, a)
                    act.wait_ge(s_ss, a)
                f(qk[:, 0], bQK[:, 0:C].rearrange("p (h x d) -> p x h d", h=HP, x=HX), ACT.Silu)
                f(qk[:, 1], bQK[:, C:2 * C].rearrange("p (h x d) -> p x h d", h=HP, x=HX), ACT.Silu).then_inc(s_qks, 1)
                act.wait_ge(s_vb, a + 1)
                act.wait_ge(s_z, a + 1)
                if old(0, a if not isinstance(a, int) else a - 1):
                    act.wait_ge(s_vn, a)
                f(v[:, :, :, :].rearrange("p h x d -> p (h x d)"), bA[:, 0:C], ACT.Silu).then_inc(s_vs, 1)
                act.wait_ge(s_qks, a + 1)
                f(sq[:, :, :, :, :].rearrange("p t x h d -> p (t x h d)"), qk[:, :, :, :, :].rearrange("p t x h d -> p (t x h d)"),
                  ACT.Square).then_inc(s_sq, 1)

            def A_inv(a):
                nc.scalar.preload_act_table_set(LN_EXP)
                act.wait_ge(s_z, a + 1)
                chained(f(ez[:, :], zc[:, :], ACT.Exp, scale=-1.0))
                act.wait_ge(s_ss, a + 1)
                if old(0, a if not isinstance(a, int) else a - 1):
                    act.wait_ge(s_inv, a)
                f(lns[:, 24:36], ez[:, :], ACT.Ln, bias=one[:, 0:1])
                chained(f(lns[:, 0:24], ss[:, :], ACT.Ln, bias=eps6[:, 0:1]))
                if old(0, a if not isinstance(a, int) else a - 1):
                    act.wait_ge(s_kn, a)
                    act.wait_ge(s_qn, a)
                    act.wait_ge(s_vn, a)
                f(inv[:, :], lns[:, :], ACT.Exp, scale=-0.5).then_inc(s_inv, 1)

            def place(a, par, half):
                if half == 0:
                    act.wait_ge(s_vT, a + 1)
                if old(0, a if not isinstance(a, int) else a - 1):
                    act.wait_ge(s_state, a * 2 - 1 + half)
                lo = half * (T // 2)
                f(Pr[:, :, lo:lo + T // 2, :, D], vT[:, par, :, :, lo:lo + T // 2].rearrange("p h b i -> p b i h"),
                  ACT.Copy, scale=-1.0).then_inc(s_place, 1)

            def Fa_oc(q):
                act.wait_ge(s_ocp, q + 1)
                f(oc0[:, :], bFa[:, 0:P], ACT.Copy)
                f(oc1[:, :], bFa[0:C1, P:2 * P], ACT.Copy).then_inc(s_oc, 1)

            def Fa_h(q):
                act.wait_ge(s_nm2, q + 1)
                if old(0, q if not isinstance(q, int) else q - 1):
                    act.wait_ge(s_h2Tp, q)
                f(h2[:, :], xh[:, bass.ds(q, 1), :].rearrange("p z c -> p (z c)"), ACT.Identity, scale=rstd2[:, 0:1],
                  bias=nmr2[:, 0:1]).then_inc(s_h2, 1)

            def Fa_hT(q, fp):
                act.wait_ge(s_h2Tp, q + 1)
                if old(0, q if not isinstance(q, int) else q - 2):
                    act.wait_ge(s_up, q * UN - UN)
                f(h2T0[:, fp], bFa[:, 0:P], ACT.Copy)
                f(h2T1[:, fp], bFa[0:C1, P:2 * P], ACT.Copy).then_inc(s_h2T, 1)

            def Fa_exp(q):
                act.wait_ge(s_nmx, q + 1)
                if old(0, q if not isinstance(q, int) else q - 1):
                    act.wait_ge(s_gate, q)
                f(prob[:, 0:E], bFa[:, 0:E], ACT.Exp, bias=negmax[:, 0:1])
                f(prob[:, E:E + 1], bFa[:, E:E + 1], ACT.Exp, scale=-1.0, bias=neg_sgb[:, 0:1]).then_inc(s_pr, 1)

            def unit(q, fp, m):
                act.wait_ge(s_up, q * UN + (m + 1))
                if m >= RING or not isinstance(q, int) or q >= 1:
                    act.wait_ge(s_hid, q * UN + (m + 1 - RING))
                if m == 0:
                    act.wait_ge(s_gate, q + 1)
                f(sg[:, m % RING], bUp[m % 2][:, 0:H], ACT.Silu)
                f(ug[:, m % RING], bUp[m % 2][:, H:2 * H], ACT.Copy, scale=gate[:, fp, m:m + 1]).then_inc(s_ug, 1)

            def hidden(q, g):
                lo, hi = GRP[g]
                act.wait_ge(s_ht, q * NG + (g + 1))
                if g >= 2:
                    act.wait_ge(s_dg, q * NG + (g - 1))
                elif g == 0 and (not isinstance(q, int) or q >= 1):
                    act.wait_ge(s_dg, q * NG)
                w = (hi - lo) * P
                f(hidT[:, turn_bank(g)].rearrange("p k t -> p (k t)")[:, 0:w], bHt[turn_bank(g)][:, 0:w], ACT.Copy).then_inc(s_htc, 1)

            def Fc_out(q):
                act.wait_ge(s_outp, q + 1)
                at = q * T
                f(xT0[:, :, bass.ds(at, T)], bDn[:, 0:P].rearrange("c (b t) -> c b t", b=NB), ACT.Copy)
                f(xT1[:, :, bass.ds(at, T)], bDn[0:C1, P:2 * P].rearrange("c (b t) -> c b t", b=NB), ACT.Copy).then_inc(s_outc, 1)

            def step(c, par, on):
                X_, A, A2, R, Fa, Fb, Fc = (on.get(k) for k in ("X", "A", "A2", "R", "Fa", "Fb", "Fc"))
                if n[0]:
                    act.sem_clear(s_act)
                    n[0] = 0

                def do(q, fn, *args):
                    if q is not None:
                        fn(q, *args)

                def units(*ms):
                    for m in ms:
                        do(Fb, unit, par, m)

                def hT(g):
                    do(Fb, hidden, g)

                do(R, place, par, 1)
                do(A, A_h)
                units(0)
                do(A, A_hT)
                units(1)
                do(Fc, Fc_out)
                do(A, A_silu)
                units(2)
                do(X_, A_xs)
                units(3)
                do(Fa, Fa_oc)
                hT(0)
                units(4, 5, 6)
                do(Fa, Fa_h)
                do(Fa, Fa_hT, 1 - par)
                hT(1)
                do(A2, place, 1 - par, 0)
                units(7)
                do(A, A_inv)
                if isinstance(c, int) and Fa == 0:
                    act.wait_ge(s_sgb, 1)
                do(Fa, Fa_exp)
                units(8)
                hT(2)
                units(9, 10, 11)
                hT(3)
                hT(4)

            act.wait_ge(s_x, 32)
            act.wait_ge(s_const, 4)
            chunks(act, step)

        @block.gpsimd
        def _(pool):
            tt = nc.gpsimd.tensor_tensor
            n = [0]

            def chained(ins):
                n[0] += 1
                ins.then_inc(s_pool, 1)
                pool.wait_ge(s_pool, n[0])

            def rstd(a, ready, mv, ve, out_, eps, done, used):
                pool.wait_ge(ready, a + 1)
                if old(0, a if not isinstance(a, int) else a - 1):
                    pool.wait_ge(used, a)
                chained(tt(ve[:, :], mv[:, 1:2], eps[:, :], ALU.add))
                tt(out_[:, :], ve[:, :], neg_half[:, :], ALU.pow).then_inc(done, 1)

            def A_norm(a):
                pool.wait_ge(s_inv, a + 1)
                if old(0, a if not isinstance(a, int) else a - 1):
                    pool.wait_ge(s_scr, a * 128)
                    pool.wait_ge(s_vT, a)
                tt(kqn[:, 1].rearrange("p x (h d) -> p (x h) d", d=D), qk[:, 0].rearrange("p x h d -> p (x h) d"),
                   inv[:, 0:12].unsqueeze(2).to_broadcast([P, NH, D]), ALU.mult).then_inc(s_qn, 1)
                pool.wait_ge(s_vs, a + 1)
                tt(vn[:, :, :, :].rearrange("p h x d -> p (h x) d"), v[:, :, :, :].rearrange("p h x d -> p (h x) d"),
                   inv[:, 24:36].unsqueeze(2).to_broadcast([P, NH, D]), ALU.mult).then_inc(s_vn, 1)

            def out_half(c, par, half):
                products(c, par, half)
                sums(c, half, 8)
                rest(c, half)

            def products(c, par, half):
                pool.wait_ge(s_state, c * 2 + (half + 1))
                if half == 0:
                    pool.wait_ge(s_QB[par], loads(c, par))
                if half or not isinstance(c, int) or c > 0:
                    pool.wait_ge(s_oT, c * 2 + half)
                lo = half * (T // 2)
                tt(PQ[:, :, :].rearrange("p (i b h) d -> p i b (h d)", i=T // 2, b=BR),
                   SH[:, par, lo:lo + T // 2].rearrange("p i b h d -> p i b (h d)"),
                   QB[:, par, :, lo:lo + T // 2].rearrange("p b i h d -> p i b (h d)"), ALU.mult).then_inc(s_pq, 1)
                pool.wait_ge(s_pq, c * 2 + (half + 1))

            def sums(c, half, w):
                chained(tt(PQ[:, :, 0:w], PQ[:, :, 0:w], PQ[:, :, w:2 * w], ALU.add))

            def rest(c, half):
                lo = half * (T // 2)
                sums(c, half, 4)
                sums(c, half, 2)
                if half == 0 and old(0, c if not isinstance(c, int) else c - 1):
                    pool.wait_ge(s_otok, c)
                s = PQ[:, :, 0:2].rearrange("p (i b h) d -> p i b h d", i=T // 2, b=BR)
                tt(oT[:, :, :, lo:lo + T // 2].rearrange("p h b i -> p i b h"), s[:, :, :, :, 0], s[:, :, :, :, 1],
                   ALU.add).then_inc(s_oT, 1)

            def hidden(q, m):
                pool.wait_ge(s_ug, q * UN + (m + 1))
                if m == 0 and (not isinstance(q, int) or q >= 1):
                    pool.wait_ge(s_ht, q * NG)
                tt(hid[:, m * H:(m + 1) * H], sg[:, m % RING], ug[:, m % RING], ALU.mult).then_inc(s_hid, 1)

            def step(c, par, on):
                X_, A2, R, Fa, Fb = (on.get(k) for k in ("X", "A2", "R", "Fa", "Fb"))
                if n[0]:
                    pool.sem_clear(s_pool)
                    n[0] = 0

                def do(q, fn, *args):
                    if q is not None:
                        fn(q, *args)

                def units(*ms):
                    for m in ms:
                        do(Fb, hidden, m)

                do(A2, A_norm)
                do(Fa, products, 1 - par, 1)
                do(Fa, sums, 1, 8)
                do(Fa, rest, 1)
                units(0, 1, 2, 3, 4)
                do(Fa, rstd, s_st2, mv2, ve2, rstd2, eps5, s_rs2, s_h2)
                units(5)
                do(R, products, par, 0)
                units(6, 7)
                do(R, sums, 0, 8)
                units(8)
                do(X_, rstd, s_st1, mv1, ve1, rstd1, eps6, s_rs1, s_h)
                units(9)
                do(R, rest, 0)
                units(10, 11)

            pool.memset(ident[:, :], 0.0).then_inc(s_id, 1)
            pool.wait_ge(s_id, 1)
            pool.affine_select(out=ident[:, :], in_=ident[:, :], compare_op=ALU.not_equal, fill=1.0, base=0,
                               pattern=[[-1, P]], channel_multiplier=1).then_inc(s_id, 1)
            for t, val in ((neg_half, -0.5), (eps6, 1e-6), (eps5, 1e-5), (one, 1.0)):
                pool.memset(t[:, :], val).then_inc(s_const, 1)
            pool.memset(lower[:, :, :], 1.0).then_inc(s_low, 1)
            pool.wait_ge(s_low, 1)
            pool.affine_select(out=lower[:, :, :], in_=lower[:, :, :], compare_op=ALU.is_gt, fill=0.0, base=0,
                               pattern=[[1, E], [-1, E]], channel_multiplier=0).then_inc(s_low, 1)
            pool.memset(SH[:, 1, T - 1], 0.0).then_inc(s_zero, 1)
            pool.wait_ge(s_const, 4)
            chunks(pool, step)

        @block.vector
        def _(dve):
            tt, ts = nc.vector.tensor_tensor, nc.vector.tensor_scalar
            n = [0]

            def count(ins):
                n[0] += 1
                ins.then_inc(s_chain, 1)
                return s_chain, n[0]

            def stats(src, st, mv, done):
                dve.wait_ge(*count(nc.vector.bn_stats(st[:, :], src)))
                nc.vector.bn_aggr(mv[:, :], st[:, :]).then_inc(done, 1)

            def A_stats(a):
                dve.wait_ge(s_xT, a + 1)
                if old(0, a if not isinstance(a, int) else a - 1):
                    dve.wait_ge(s_rs1, a)
                    dve.wait_ge(s_nm1, a)
                stats(bA[:, 0:C], st1, mv1, s_st1)

            def nmr(a, mv, rs, out_, rs_ready, used, done):
                dve.wait_ge(rs_ready, a + 1)
                if old(0, a if not isinstance(a, int) else a - 1):
                    dve.wait_ge(used, a)
                nc.vector.scalar_tensor_tensor(out=out_[:, :], in0=mv[:, 0:1], scalar=-1.0, in1=rs[:, :], op0=ALU.mult,
                                               op1=ALU.mult).then_inc(done, 1)

            def A_xh(a):
                dve.wait_ge(s_h, a + 1)
                tt(xh[:, bass.ds(a, 1), :].rearrange("p z c -> p (z c)"), bA[:, 0:C], h[:, :], ALU.add).then_inc(s_xh, 1)

            def A_z(a):
                dve.wait_ge(s_vb, a + 1)
                if old(0, a if not isinstance(a, int) else a - 1):
                    dve.wait_ge(s_inv, a)
                ts(zc[:, :], bA[:, C:C + NH], -40.0, None, ALU.max).then_inc(s_z, 1)

            def A_ss(a):
                dve.wait_ge(s_sq, a + 1)
                if old(0, a if not isinstance(a, int) else a - 1):
                    dve.wait_ge(s_inv, a)
                nc.vector.tensor_reduce(ss[:, :], sq[:, :, :, :, :].rearrange("p t x h d -> p (t x h) d"), X, ALU.add).then_inc(s_ss, 1)

            def A_kn(a):
                dve.wait_ge(s_inv, a + 1)
                if old(0, a if not isinstance(a, int) else a - 1):
                    dve.wait_ge(s_scr, a * 128)
                w = count(tt(ksc[:, :, :], inv[:, 12:24].rearrange("p (x h) -> p x h", x=HX),
                             inv[:, 24:36].rearrange("p (h x) -> p x h", x=HX), ALU.mult))
                dve.wait_ge(*w)
                tt(kqn[:, 0].rearrange("p x (h d) -> p (x h) d", d=D), qk[:, 1].rearrange("p x h d -> p (x h) d"),
                   ksc[:, :, :].rearrange("p x h -> p (x h)").unsqueeze(2).to_broadcast([P, NH, D]), ALU.mult).then_inc(s_kn, 1)

            def A_vT(a, par):
                dve.wait_ge(s_vn, a + 1)
                if old(0, a if not isinstance(a, int) else a - 2):
                    dve.wait_ge(s_place, a * 2 - 2)
                nc.vector.transpose(vT[:, par].rearrange("p h b i -> p (h b i)"), vn[:, :, :, :].rearrange("p h x d -> p (h x d)")).then_inc(s_vT, 1)

            def Fa_otok(q):
                dve.wait_ge(s_oT, q * 2 + 2)
                if old(0, q if not isinstance(q, int) else q - 1):
                    dve.wait_ge(s_ocp, q)
                nc.vector.transpose(otok[:, :], oT[:, :, :, :].rearrange("p h b i -> p (h b i)")).then_inc(s_otok, 1)

            def Fa_x1(q):
                dve.wait_ge(s_y, q + 1)
                if old(0, q if not isinstance(q, int) else q - 1):
                    dve.wait_ge(s_rs2, q)
                    dve.wait_ge(s_nm2, q)
                xq = xh[:, bass.ds(q, 1), :].rearrange("p z c -> p (z c)")
                dve.wait_ge(*count(tt(xq, bFa[:, 0:C], xq, ALU.add)))
                stats(xq, st2, mv2, s_st2)

            def Fa_max(q):
                dve.wait_ge(s_lg, q + 1)
                nc.vector.tensor_reduce(negmax[:, :], bFa[:, 0:E], X, ALU.max, negate=True).then_inc(s_nmx, 1)

            def Fa_gates(q, fp):
                pe_, po = prob[:, 0:E].unsqueeze(2).to_broadcast([P, E, E]), prob[:, 0:E].unsqueeze(1).to_broadcast([P, E, E])
                w = {}
                def rank1():
                    dve.wait_ge(s_pr, q + 1)
                    if old(0, q if not isinstance(q, int) else q - 2):
                        dve.wait_ge(s_ug, q * UN - UN)
                    count(tt(gt[:, :, :], po, pe_, ALU.is_gt))
                    w["eq"] = count(tt(eq[:, :, :], po, pe_, ALU.is_equal))
                    count(ts(den[:, 1:2], prob[:, E:E + 1], 1.0, None, ALU.add))
                def rank2():
                    dve.wait_ge(*w["eq"])
                    w["eq"] = count(tt(eq[:, :, :], eq[:, :, :], lower[:, :, :], ALU.mult))
                def rank3():
                    dve.wait_ge(*w["eq"])
                    w["gt"] = count(tt(gt[:, :, :], gt[:, :, :], eq[:, :, :], ALU.add))
                def rank4():
                    dve.wait_ge(*w["gt"])
                    w["rank"] = count(nc.vector.tensor_reduce(rank[:, :], gt[:, :, :], X, ALU.add))
                def pick():
                    dve.wait_ge(*w["rank"])
                    w["sel"] = count(nc.vector.scalar_tensor_tensor(out=sel[:, :], in0=rank[:, :], scalar=2.0, in1=prob[:, 0:E],
                                                                    op0=ALU.is_lt, op1=ALU.mult))
                def total():
                    dve.wait_ge(*w["sel"])
                    w["den"] = count(nc.vector.tensor_reduce(den[:, 0:1], sel[:, :], X, ALU.add))
                def recip():
                    dve.wait_ge(*w["den"])
                    w["rden"] = count(nc.vector.reciprocal(rden[:, :], den[:, :]))
                def coefs():
                    dve.wait_ge(*w["rden"])
                    w["om"] = count(ts(coef[:, :], rden[:, 1:2], -1.0, 1.0, ALU.mult, ALU.add))
                    count(ts(gate[:, fp, E:UN], one[:, 0:1].to_broadcast([P, UN - E]), rden[:, 1:2], None, ALU.mult))
                def coef2():
                    dve.wait_ge(*w["om"])
                    w["co"] = count(tt(coef[:, :], coef[:, :], rden[:, 0:1], ALU.mult))
                def last():
                    dve.wait_ge(*w["co"])
                    ts(gate[:, fp, 0:E], sel[:, :], coef[:, 0:1], None, ALU.mult).then_inc(s_gate, 1)
                return [rank1, rank2, rank3, rank4, pick, total, recip, coefs, coef2, last]

            def Fc_res(q):
                dve.wait_ge(s_dg, q * NG + NG)
                if old(0, q if not isinstance(q, int) else q - 1):
                    dve.wait_ge(s_outp, q)
                xq = xh[:, bass.ds(q, 1), :].rearrange("p z c -> p (z c)")
                tt(res[:, :], bDn[:, 0:C], xq, ALU.add).then_inc(s_res, 1)

            def step(c, par, on):
                X_, A, A2, R, Fa, Fb, Fc = (on.get(k) for k in ("X", "A", "A2", "R", "Fa", "Fb", "Fc"))
                work = []

                def at(slot, q, fn, *args):
                    if q is not None:
                        work.append((slot, lambda: fn(q, *args)))

                at(2, A2, A_kn)
                at(9, A, A_xh)
                at(12, Fc, Fc_res)
                at(18, A, A_z)
                at(20, A2, A_vT, 1 - par)
                at(24, Fa, Fa_otok)
                at(26, A, A_ss)
                at(36, Fa, Fa_x1)
                at(40, Fa, nmr, mv2, rstd2, nmr2, s_rs2, s_h2, s_nm2)
                at(50, Fa, Fa_max)
                at(53, X_, A_stats)
                if Fa is not None:
                    for i, g in enumerate(Fa_gates(Fa, 1 - par)):
                        work.append((54 + i, g))
                at(64, X_, nmr, mv1, rstd1, nmr1, s_rs1, s_h, s_nm1)
                work.sort(key=lambda w: w[0])

                def fill(slot):
                    while work and work[0][0] <= slot:
                        work.pop(0)[1]()

                if R is not None:
                    dve.wait_ge(s_KB[par], loads(c, par))
                    Sb = [None, None]
                    for i in range(T):
                        prev = SH[:, 1 - par, T - 1] if i == 0 else SH[:, par, i - 1]
                        slot = 4 * i
                        if i % (T // 2) == 0:
                            dve.wait_ge(s_place, c * 2 + (i // (T // 2) + 1))
                            if not isinstance(c, int) or c >= 2:
                                dve.wait_ge(s_pq, c * 2 - 3 + i // (T // 2))
                        def each(fn, waits):
                            got = []
                            for br in range(BR):
                                if waits[br] is not None:
                                    dve.wait_ge(*waits[br])
                                got.append(fn(br))
                            return got
                        w = each(lambda br: count(tt(Pr[:, br, i, :, 0:D], prev[:, br], KB[:, par, br, i], ALU.mult)), Sb)
                        fill(slot)
                        w = each(lambda br: count(nc.vector.tensor_reduce(u[:, i % 2, br], Pr[:, br, i], X, ALU.add, negate=True)), w)
                        fill(slot + 1)
                        w = each(lambda br: count(tt(TT[:, i % 2, br], KB[:, par, br, i],
                                                     u[:, i % 2, br].unsqueeze(2).to_broadcast([P, HP, D]), ALU.mult)), w)
                        fill(slot + 2)
                        def grow(br):
                            ins = tt(SH[:, par, i, br], prev[:, br], TT[:, i % 2, br], ALU.add)
                            if i % (T // 2) == T // 2 - 1 and br == BR - 1:
                                ins.then_inc(s_state, 1)
                                return s_state, c * 2 + (i // (T // 2) + 1)
                            return count(ins)
                        Sb = each(grow, w)
                        fill(slot + 3)
                fill(1000)
                dve.wait_ge(s_chain, n[0]) if n[0] else None
                if R is not None:
                    dve.wait_ge(s_state, c * 2 + 2)
                if n[0]:
                    dve.sem_clear(s_chain)
                n[0] = 0

            dve.wait_ge(s_const, 4)
            dve.wait_ge(s_low, 2)
            dve.wait_ge(s_zero, 1)
            dve.wait_ge(s_wr, 80)
            ts(neg_sgb[:, :], sgb[:, :], -1.0, None, ALU.mult).then_inc(s_sgb, 1)
            chunks(dve, step)


_INS = ['x', 'L0_conv_Wq', 'L0_conv_Wk', 'L0_conv_Wv', 'L0_conv_Wb', 'L0_conv_Wo', 'L0_ffn_router_w', 'L0_ffn_w_gate',
        'L0_ffn_w_up', 'L0_ffn_w_down', 'L0_ffn_ws_gate', 'L0_ffn_ws_up', 'L0_ffn_ws_down', 'L0_ffn_sg_w', 'L0_ffn_sg_b']


def kernel(**inputs):
    import numpy as _np
    import concourse.bacc as _bacc
    from concourse import mybir as _mybir
    from concourse.bass_utils import run_bass_kernel_spmd as _run

    nc = _bacc.Bacc("TRN2", target_bir_lowering=False, num_devices=1)
    arrays, args = {}, []
    for name in _INS:
        a = _np.ascontiguousarray(inputs[name])
        shape = (NB, C, L) if name == 'x' else a.shape
        a = a.reshape(shape)
        arrays[f"in_{name}_dram"] = a
        args.append(nc.dram_tensor(f"in_{name}_dram", a.shape, _mybir.dt.from_np(a.dtype), kind="ExternalInput").ap())
    o = nc.dram_tensor("out_0_dram", (NB, C, L), _mybir.dt.float32, kind="ExternalOutput").ap()
    build(nc, *args, o)
    r = _run(nc, [arrays], core_ids=[0])
    return r.results[0]["out_0_dram"].reshape(NB, C, 16, 16)
```

```python
import concourse.bass as bass
from concourse import mybir
from contextlib import ExitStack

F32, F32R = mybir.dt.float32, mybir.dt.float32r
ALU = mybir.AluOpType
ACT = mybir.ActivationFunctionType
X = mybir.AxisListType.X

NB, C, L = 8, 192, 256
NH, D = 12, 16
T = 16
NC = L // T
P = 128
C0, C1 = P, C - P
BP, BR, HP, HX = 4, 2, 6, 2
G = HP * D
E, H, HS = 8, 192, 768
UN = E + HS // H
HID = UN * H
KT = HID // P
GRP = [(0, 4), (4, 8), (8, 12), (12, 16), (16, 18)]
NG = len(GRP)
RING = 4
NQK, NVB = 2 * C, C + NH
EARLY = 14
FIRST = 4
LN_EXP = "natural_log_exp_and_others"


def build(nc, x, Wq, Wk, Wv, Wb, Wo, router_w, w_gate, w_up, w_down, ws_gate, ws_up, ws_down, sg_w, sg_b, out):
    ctx = ExitStack()
    with ctx:
        def sb(name, shape, dtype=F32):
            return ctx.enter_context(nc.sbuf_tensor(name, shape, dtype))

        place = {}

        def fixed(name, shape, dtype):
            place[name] = -(-nc.sbuf_base // 32) * 32, shape
            ctx.enter_context(nc.sbuf_tensor(name + "_area", shape, F32))
            return nc.alloc_sbuf_tensor_at(name, shape, dtype, offset=place[name][0])

        def view(name):
            return nc.alloc_sbuf_tensor_at(name + "_unsplit", place[name][1], F32, offset=place[name][0])

        def sem(name):
            return ctx.enter_context(nc.semaphore(name))

        kq_dram = nc.dram_tensor("kq_scratch", [NC, 2, BP, HX, BR, T, G], F32, kind="Internal").ap()

        Whi0 = sb("Whi0", [C0, UN, 2 * H], F32R)
        Wlo0, W1 = fixed("Wlo0", [P, UN, 2 * H], F32R), fixed("W1", [P, UN, 2 * H], F32R)
        raw0, raw1 = view("Wlo0"), view("W1")
        xT0 = sb("xT0", [C0, NB, L])
        xin1 = sb("xT1", [P, NB, L])
        xT1 = xin1[C1:P]
        ident = sb("ident", [P, P])
        Wp0, Wp1 = sb("Wp0", [C0, NQK + NVB]), sb("Wp1", [C1, NQK + NVB])
        Wo0, Wo1 = sb("Wo0", [C0, C]), sb("Wo1", [C1, C])
        Wr0, Wr1 = sb("Wr0", [C0, E + 1]), sb("Wr1", [C1, E + 1])
        Wd = sb("Wd", [P, KT, C])
        xh = sb("xh", [P, NC, C])
        neg_half, eps6, eps5, one = sb("neg_half", [P, 1]), sb("eps6", [P, 1]), sb("eps5", [P, 1]), sb("one", [P, 1])
        sgb, neg_sgb = sb("sgb", [P, 1]), sb("neg_sgb", [P, 1])
        lower = sb("lower", [P, E, E])
        xs0, xs = sb("xs0", [C0, NB, T]), sb("xs1", [P, NB, T])
        xs1 = xs[C1:P]
        st1, mv1 = sb("st1", [P, 6]), sb("mv1", [P, 2])
        ve1, rstd1, nmr1 = sb("ve1", [P, 1]), sb("rstd1", [P, 1]), sb("nmr1", [P, 1])
        rstd_1 = sb("rstd_1", [P, 1])
        h = sb("h", [P, C])
        hT0, hT1 = sb("hT0", [C0, P]), sb("hT1", [C1, P])
        zc = sb("zc", [P, NH])
        qk = sb("qk", [P, 2, HX, HP, D])
        sq = sb("sq", [P, 2, HX, HP, D])
        v = sb("v", [P, HP, HX, D])
        ss, ez, lns, inv = sb("ss", [P, 24]), sb("ez", [P, NH]), sb("lns", [P, 36]), sb("inv", [P, 36])
        ksc = sb("ksc", [P, HX, HP])
        kqn = sb("kqn", [P, 2, HX, G])
        vn = sb("vn", [P, HP, HX, D])
        vT = sb("vT", [P, 2, HP, BR, T])
        KB = sb("KB", [P, BR, T, HP, D])
        QB = sb("QB", [P, BR, T, HP, D])
        Pr = sb("Pr", [P, BR, T, HP, D + 1])
        u = sb("u", [P, 2, BR, HP])
        TT = sb("TT", [P, 2, BR, HP, D])
        SH = sb("SH", [P, T, BR, HP, D])
        PQ = sb("PQ", [P, T // 2 * BR * HP, D])
        oT = sb("oT", [P, HP, BR, T])
        otok = sb("otok", [P, C])
        oc0, oc1 = sb("oc0", [C0, P]), sb("oc1", [C1, P])
        st2, mv2 = sb("st2", [P, 6]), sb("mv2", [P, 2])
        ve2, rstd2, nmr2 = sb("ve2", [P, 1]), sb("rstd2", [P, 1]), sb("nmr2", [P, 1])
        h2 = sb("h2", [P, C])
        h2T = sb("h2T", [P, 2 * P])
        hiT, loT = sb("hiT", [P, 2, 2 * P], F32R), sb("loT", [P, 2, 2 * P], F32R)
        negmax, prob = sb("negmax", [P, 1]), sb("prob", [P, E + 1])
        gt, eq, rank = sb("gt", [P, E, E]), sb("eq", [P, E, E]), sb("rank", [P, E])
        sel, den, rden, coef = sb("sel", [P, E]), sb("den", [P, 2]), sb("rden", [P, 2]), sb("coef", [P, 1])
        gate = sb("gate", [P, 2, UN])
        sg, ug = sb("sg", [P, RING, H]), sb("ug", [P, RING, H])
        hid = sb("hid", [P, HID // 2])
        hidT = sb("hidT", [P, 2, 4, P])
        res = sb("res", [P, C])

        bank = [ctx.enter_context(nc.psum_tensor(f"bank{i}", [P, 512], F32)) for i in range(8)]
        bA, bQK, bFa, bDn = bank[0], bank[1], bank[2], bank[3]
        bUp, bHt = bank[4:6], bank[6:8]

        s_whi, s_wlo0, s_w1, s_clear = (sem(n) for n in (
            "weights_hi_ready", "weights_lo0_ready", "weights_1_ready", "zeros_ready"))
        s_split = sem("tokens_split")
        s_wp, s_wo, s_wr, s_wd = (sem(n) for n in ("wp_in", "wo_in", "wr_in", "wd_in"))
        s_wu = [sem("up_weights0_in"), sem("up_weights1_in")]
        s_x = [sem("x_first_in"), sem("x_rest_in")]
        s_const, s_zero, s_id, s_low = sem("consts_ready"), sem("state_zero"), sem("ident_ready"), sem("lower_ready")
        s_sgb = sem("sgb_ready")
        s_chain = sem("dve_chain")
        s_pool = sem("pool_chain")
        s_act = sem("act_chain")
        s_xs, s_xT, s_st1, s_rs1, s_nm1, s_h, s_xh = (sem(n) for n in (
            "xs_ready", "xT_ready", "stats1_ready", "rstd1_ready", "nmr1_ready", "h_ready", "xh_ready"))
        s_hTp, s_hT, s_qk, s_vb, s_z, s_qks, s_vs, s_sq, s_ss, s_inv = (sem(n) for n in (
            "hT_psum_ready", "hT_ready", "qk_ready", "vb_ready", "z_ready", "qk_silu_ready", "v_silu_ready",
            "squares_ready", "norms_ready", "inv_ready"))
        s_kn, s_qn, s_vn, s_vT, s_place = (sem(n) for n in (
            "k_normed", "q_normed", "v_normed", "vT_ready", "v_placed"))
        s_scr = sem("scratch_written")
        s_KB, s_QB = [sem("KB_half0_in"), sem("KB_half1_in")], [sem("QB_half0_in"), sem("QB_half1_in")]
        s_state, s_pq, s_oT = sem("states_ready"), sem("states_read"), sem("o_summed")
        s_otok, s_ocp, s_oc, s_y, s_st2, s_rs2, s_nm2, s_h2 = (sem(n) for n in (
            "o_by_token", "oc_psum_ready", "oc_ready", "y_ready", "stats2_ready", "rstd2_ready", "nmr2_ready", "h2_ready"))
        s_h2Tp, s_h2T, s_lg, s_nmx, s_pr, s_gate = (sem(n) for n in (
            "h2T_psum_ready", "h2T_ready", "logits_ready", "negmax_ready", "probs_ready", "gates_ready"))
        s_up, s_ug, s_hid = sem("up_ready"), sem("unit_copied"), sem("hidden_ready")
        s_ht, s_htc, s_dg = sem("hidT_psum_ready"), sem("hidT_ready"), sem("down_group_done")
        s_rs_1, s_x1 = sem("one_plus_rstd1_ready"), sem("x1_ready")
        s_res, s_outp, s_outc, s_out = sem("res_ready"), sem("outT_psum_ready"), sem("out_copied"), sem("out_written")

        block = ctx.enter_context(nc.Block())

        def chunks(eng, step):
            def stages(c):
                return dict(X=c + 3, A=c + 2, A2=c + 1, R=c, Fa=c - 1, Fb=c - 2, Fc=c - 3)
            def edge(c):
                step(c, c % 2, {k: n for k, n in stages(c).items() if 0 <= n < NC})
            for c in range(-3, 4):
                edge(c)
            with eng.Fori(0, 4) as k:
                for j in range(2):
                    c = eng.snap(k * 2 + (4 + j))
                    step(c, j, stages(c))
            for c in range(12, NC + 3):
                edge(c)

        def old(w, n):
            return not isinstance(n, int) or n >= 0

        free = [b[:, i * 2 * H:(i + 1) * 2 * H] for b, n in (
            (hid[:, :], 3), (sg[:, :, :].rearrange("p r h -> p (r h)"), 2), (ug[:, :, :].rearrange("p r h -> p (r h)"), 2),
            (hidT[:, :, :, :].rearrange("p a k t -> p (a k t)"), 2)) for i in range(n)]

        def turn_bank(g):
            return g % 2

        @block.sync
        def _(sp):
            def scratch(a):
                sp.wait_ge(s_kn, a + 1)
                sp.wait_ge(s_qn, a + 1)
                for t in range(2):
                    for bp in range(BP):
                        sp.dma_start(kq_dram[bass.ds(a, 1), t, bp].rearrange("z x b i g -> (b i) (z x) g"),
                                     kqn[32 * bp:32 * bp + 32, t]).then_inc(s_scr, 16)

            def spread(a):
                sp.wait_ge(s_scr, (a + 1) * 128)
                for half in range(2):
                    lo, hi = half * (T // 2), (half + 1) * (T // 2)
                    for t, B, arrived, read, n in ((0, KB, s_KB, s_state, 1), (1, QB, s_QB, s_pq, 2)):
                        if old(0, a if not isinstance(a, int) else a - 1):
                            sp.wait_ge(read, a * (2 * n) - n + n * half)
                        for br in range(BR):
                            sp.dma_start(B[:, br, lo:hi].rearrange("p i h d -> p (i h d)"),
                                         kq_dram[bass.ds(a, 1), t, :, :, br, lo:hi].rearrange("z b x i g -> (z b x) (i g)")
                                         .unsqueeze(1).to_broadcast([BP * HX, D, T // 2 * G])).then_inc(arrived[half], 16)

            def load_x(i, lo, hi):
                sp.dma_start(xT0[:, :, lo:hi], x[:, 0:C0, lo:hi].rearrange("b c l -> c b l")).then_inc(s_x[i], 16)
                sp.dma_start(xT1[:, :, lo:hi], x[:, C0:C, lo:hi].rearrange("b c l -> c b l")).then_inc(s_x[i], 16)

            def load_up(i, to, lo, hi):
                for half, we, ws in ((0, w_gate, ws_gate), (H, w_up, ws_up)):
                    sp.dma_start(to[:, 0:E, half:half + H], we[:, lo:hi, :].rearrange("e c h -> c e h")).then_inc(s_wu[i], 16)
                    sp.dma_start(to[:, E:UN, half:half + H], ws[lo:hi, :].rearrange("c (s h) -> c s h", h=H)).then_inc(s_wu[i], 16)

            def store(lo, hi):
                sp.dma_start(out[:, 0:C0, lo:hi].rearrange("b c l -> c b l"), xT0[:, :, lo:hi]).then_inc(s_out, 16)
                sp.dma_start(out[:, C0:C, lo:hi].rearrange("b c l -> c b l"), xT1[:, :, lo:hi]).then_inc(s_out, 16)

            def load():
                load_x(0, 0, FIRST * T)
                for i, w in enumerate((Wq, Wk, Wv)):
                    sp.dma_start(Wp0[:, i * C:i * C + C], w[0:C0, :]).then_inc(s_wp, 16)
                    sp.dma_start(Wp1[:, i * C:i * C + C], w[C0:C, :]).then_inc(s_wp, 16)
                sp.dma_start(Wp0[:, 3 * C:3 * C + NH], Wb[0:C0, :]).then_inc(s_wp, 16)
                sp.dma_start(Wp1[:, 3 * C:3 * C + NH], Wb[C0:C, :]).then_inc(s_wp, 16)
                sp.dma_start(Wo0[:, :], Wo[0:C0, :]).then_inc(s_wo, 16)
                sp.dma_start(Wo1[:, :], Wo[C0:C, :]).then_inc(s_wo, 16)
                sp.dma_start(Wr0[:, 0:E], router_w[0:C0, :]).then_inc(s_wr, 16)
                sp.dma_start(Wr1[:, 0:E], router_w[C0:C, :]).then_inc(s_wr, 16)
                sp.dma_start(Wr0[:, E:E + 1], sg_w[0:C0, :]).then_inc(s_wr, 16)
                sp.dma_start(Wr1[:, E:E + 1], sg_w[C0:C, :]).then_inc(s_wr, 16)
                sp.dma_start(sgb[:, :], sg_b.rearrange("(a n) -> a n", a=1).to_broadcast([P, 1])).then_inc(s_wr, 16)
                load_up(0, raw0, 0, C0)

            def load_later():
                load_x(1, FIRST * T, L)
                load_up(1, raw1[0:C1], C0, C)
                load_up(1, raw1[C1:P], C0, C)
                ke = E * H // P
                sp.dma_start(Wd[:, 0:ke, :], w_down.rearrange("e h c -> (e h) c").rearrange("(k p) c -> p k c", p=P)).then_inc(s_wd, 16)
                sp.dma_start(Wd[:, ke:KT, :], ws_down.rearrange("(k p) c -> p k c", p=P)).then_inc(s_wd, 16)

            def step(c, par, on):
                if "A2" in on:
                    scratch(on["A2"])
                    spread(on["A2"])
                if isinstance(c, int) and c == -1:
                    load_later()
                if isinstance(c, int) and on.get("Fc") == EARLY:
                    sp.wait_ge(s_outc, EARLY)
                    store(0, EARLY * T)

            load()
            chunks(sp, step)
            sp.wait_ge(s_outc, NC)
            store(EARLY * T, L)
            sp.wait_ge(s_out, 64)

        @block.tensor
        def _(pe):
            mm, tr = nc.tensor.matmul, nc.tensor.transpose

            def project(dst, a0, a1, w0, w1):
                mm(dst, a0, w0, start=True, stop=False)
                return mm(dst, a1, w1, start=False, stop=True)

            def turn(b, src):
                tr(b[:, 0:P], src[:, 0:C0], ident[:, :])
                return tr(b[0:C1, P:2 * P], src[:, C0:C], ident[:, :])

            def A_x(a):
                pe.wait_ge(s_xs, a + 1)
                if old(0, a if not isinstance(a, int) else a - 1):
                    pe.wait_ge(s_z, a)
                    pe.wait_ge(s_vs, a)
                tr(bA[:, 0:C0], xs0[:, :, :].rearrange("c b t -> c (b t)"), ident[:, :])
                tr(bA[:, C0:C], xs1.rearrange("c b t -> c (b t)"), ident[C1:P, C1:P]).then_inc(s_xT, 1)

            def A_h(a):
                pe.wait_ge(s_xh, a + 1)
                turn(bA, h).then_inc(s_hTp, 1)

            def A_proj(a, first=False):
                if first:
                    pe.wait_ge(s_wp, 8 * 16)
                pe.wait_ge(s_hT, a + 1)
                if old(0, a if not isinstance(a, int) else a - 1):
                    pe.wait_ge(s_qks, a)
                project(bQK[:, 0:NQK], hT0[:, :], hT1[:, :], Wp0[:, 0:NQK], Wp1[:, 0:NQK]).then_inc(s_qk, 1)
                project(bA[:, 0:NVB], hT0[:, :], hT1[:, :], Wp0[:, NQK:], Wp1[:, NQK:]).then_inc(s_vb, 1)

            def Fa_o(f):
                pe.wait_ge(s_otok, f + 1)
                if old(0, f if not isinstance(f, int) else f - 1):
                    pe.wait_ge(s_nmx, f)
                    pe.wait_ge(s_pr, f)
                turn(bFa, otok).then_inc(s_ocp, 1)

            def Fa_y(f, first):
                if first:
                    pe.wait_ge(s_wo, 32)
                pe.wait_ge(s_oc, f + 1)
                mm(bFa[:, 0:C], ident[:, :], xh[:, bass.ds(f, 1), :].rearrange("p z c -> p (z c)"), start=True, stop=False)
                mm(bFa[:, 0:C], oc0[:, :], Wo0[:, :], start=False, stop=False)
                mm(bFa[:, 0:C], oc1[:, :], Wo1[:, :], start=False, stop=True).then_inc(s_y, 1)

            def Fa_h(f):
                pe.wait_ge(s_h2, f + 1)
                tr(bFa[:, 0:P], h2[:, 0:C0], ident[:, :])
                tr(bFa[0:C1, P:2 * P], h2[:, C0:C], ident[:, :])
                mm(bFa[C1:P, P:2 * P], h2[:, C0:C], ident[:, :], start=True, stop=True).then_inc(s_h2Tp, 1)

            def Fa_logits(f, first):
                if first:
                    pe.wait_ge(s_wr, 80)
                pe.wait_ge(s_h2T, f + 1)
                project(bFa[:, 0:E + 1], h2T[:, 0:P], h2T[0:C1, P:2 * P], Wr0[:, :], Wr1[:, :]).then_inc(s_lg, 1)

            def Fb_up(f, fp, n, first):
                if first and n == 0:
                    pe.wait_ge(s_wlo0, UN)
                    pe.wait_ge(s_w1, UN)
                if n == 0:
                    pe.wait_ge(s_split, f + 1)
                if n >= 2 or not isinstance(f, int) or f >= 1:
                    pe.wait_ge(s_ug, f * UN + (n - 1))
                to = bUp[n % 2][:, 0:2 * H]
                mm(to, hiT[:, fp, 0:P], Whi0[:, n], start=True, stop=False)
                mm(to, hiT[:, fp, 0:P], Wlo0[:, n], start=False, stop=False)
                mm(to, loT[:, fp, 0:P], Whi0[:, n], start=False, stop=False)
                mm(to, hiT[:, fp, P:2 * P], W1[:, n], start=False, stop=False)
                mm(to, loT[0:C1, fp, P:2 * P], W1[0:C1, n], start=False, stop=True).then_inc(s_up, 1)

            def Fb_turn(f, g):
                lo, hi = GRP[g]
                pe.wait_ge(s_hid, f * UN + -(-hi * P // H))
                if g >= 2:
                    pe.wait_ge(s_htc, f * NG + (g - 1))
                elif g == 0 and (not isinstance(f, int) or f >= 1):
                    pe.wait_ge(s_htc, f * NG)
                for k in range(lo, hi):
                    last = tr(bHt[turn_bank(g)][:, (k - lo) * P:(k - lo + 1) * P], hid[:, k % (KT // 2) * P:(k % (KT // 2) + 1) * P],
                              ident[:, :])
                last.then_inc(s_ht, 1)

            def Fb_down(f, fp, g, first):
                lo, hi = GRP[g]
                if first and g == 0:
                    pe.wait_ge(s_wd, 32)
                pe.wait_ge(s_htc, f * NG + (g + 1))
                if g == 0 and (not isinstance(f, int) or f >= 1):
                    pe.wait_ge(s_outc, f)
                if g == 0:
                    pe.wait_ge(s_x1, f + 1)
                    mm(bDn[:, 0:C], ident[:, :], xh[:, bass.ds(f, 1), :].rearrange("p z c -> p (z c)"), start=True, stop=False)
                for k in range(lo, hi):
                    last = mm(bDn[:, 0:C], hidT[:, turn_bank(g), k - lo, :], Wd[:, k, :], start=False, stop=(k == KT - 1))
                last.then_inc(s_dg, 1)

            def Fc_out(f):
                pe.wait_ge(s_res, f + 1)
                turn(bDn, res).then_inc(s_outp, 1)

            def step(c, par, on):
                X_, A, Fa, Fb, Fc = (on.get(k) for k in ("X", "A", "Fa", "Fb", "Fc"))
                first = isinstance(c, int)

                def do(n, fn, *args):
                    if n is not None:
                        fn(n, *args)

                def up(*ns):
                    for n in ns:
                        do(Fb, Fb_up, par, n, first and Fb == 0)

                def ht(g):
                    do(Fb, Fb_turn, g)

                def dn(g):
                    do(Fb, Fb_down, par, g, first and Fb == 0)

                do(A, A_h)
                do(Fc, Fc_out)
                up(0, 1)
                do(A, A_proj, first and A == 0)
                up(2, 3)
                do(Fa, Fa_o)
                up(4)
                do(Fa, Fa_y, first and Fa == 0)
                ht(0)
                up(5, 6)
                dn(0)
                do(Fa, Fa_h)
                ht(1)
                up(7)
                do(X_, A_x)
                do(Fa, Fa_logits, first and Fa == 0)
                up(8)
                dn(1)
                ht(2)
                up(9, 10, 11)
                ht(3)
                dn(2)
                ht(4)
                dn(3)
                dn(4)

            pe.wait_ge(s_id, 2)
            chunks(pe, step)

        @block.scalar
        def _(act):
            f = nc.scalar.activation
            n = [0]

            def chained(ins):
                n[0] += 1
                ins.then_inc(s_act, 1)
                act.wait_ge(s_act, n[0])

            def A_xs(a):
                if old(0, a if not isinstance(a, int) else a - 1):
                    act.wait_ge(s_xT, a)
                if isinstance(a, int) and a == FIRST:
                    act.wait_ge(s_x[1], 32)
                at = a * T
                f(xs0[:, :, :], xT0[:, :, bass.ds(at, T)], ACT.Copy)
                f(xs1, xT1[:, :, bass.ds(at, T)], ACT.Copy).then_inc(s_xs, 1)

            def A_h(a):
                act.wait_ge(s_nm1, a + 1)
                f(h[:, :], bA[:, 0:C], ACT.Identity, scale=rstd1[:, 0:1], bias=nmr1[:, 0:1]).then_inc(s_h, 1)
                act.wait_ge(s_rs_1, a + 1)
                f(xh[:, bass.ds(a, 1), :].rearrange("p z c -> p (z c)"), bA[:, 0:C], ACT.Identity, scale=rstd_1[:, 0:1],
                  bias=nmr1[:, 0:1]).then_inc(s_xh, 1)

            def A_hT(a):
                act.wait_ge(s_hTp, a + 1)
                f(hT0[:, :], bA[:, 0:P], ACT.Copy)
                f(hT1[:, :], bA[0:C1, P:2 * P], ACT.Copy).then_inc(s_hT, 1)

            def A_silu(a):
                act.wait_ge(s_qk, a + 1)
                if old(0, a if not isinstance(a, int) else a - 1):
                    act.wait_ge(s_kn, a)
                    act.wait_ge(s_qn, a)
                    act.wait_ge(s_ss, a)
                f(qk[:, 0], bQK[:, 0:C].rearrange("p (h x d) -> p x h d", h=HP, x=HX), ACT.Silu)
                f(qk[:, 1], bQK[:, C:2 * C].rearrange("p (h x d) -> p x h d", h=HP, x=HX), ACT.Silu).then_inc(s_qks, 1)
                act.wait_ge(s_vb, a + 1)
                act.wait_ge(s_z, a + 1)
                if old(0, a if not isinstance(a, int) else a - 1):
                    act.wait_ge(s_vn, a)
                f(v[:, :, :, :].rearrange("p h x d -> p (h x d)"), bA[:, 0:C], ACT.Silu).then_inc(s_vs, 1)
                act.wait_ge(s_qks, a + 1)
                f(sq[:, :, :, :, :].rearrange("p t x h d -> p (t x h d)"), qk[:, :, :, :, :].rearrange("p t x h d -> p (t x h d)"),
                  ACT.Square).then_inc(s_sq, 1)

            def A_inv(a):
                nc.scalar.preload_act_table_set(LN_EXP)
                act.wait_ge(s_z, a + 1)
                chained(f(ez[:, :], zc[:, :], ACT.Exp, scale=-1.0))
                act.wait_ge(s_ss, a + 1)
                if old(0, a if not isinstance(a, int) else a - 1):
                    act.wait_ge(s_inv, a)
                f(lns[:, 24:36], ez[:, :], ACT.Ln, bias=one[:, 0:1])
                chained(f(lns[:, 0:24], ss[:, :], ACT.Ln, bias=eps6[:, 0:1]))
                if old(0, a if not isinstance(a, int) else a - 1):
                    act.wait_ge(s_kn, a)
                    act.wait_ge(s_qn, a)
                    act.wait_ge(s_vn, a)
                f(inv[:, :], lns[:, :], ACT.Exp, scale=-0.5).then_inc(s_inv, 1)

            def place(a, par, half):
                if half == 0:
                    act.wait_ge(s_vT, a + 1)
                if old(0, a if not isinstance(a, int) else a - 1):
                    act.wait_ge(s_state, a * 2 - 1 + half)
                lo = half * (T // 2)
                f(Pr[:, :, lo:lo + T // 2, :, D], vT[:, par, :, :, lo:lo + T // 2].rearrange("p h b i -> p b i h"),
                  ACT.Copy, scale=-1.0).then_inc(s_place, 1)

            def Fa_oc(q):
                act.wait_ge(s_ocp, q + 1)
                f(oc0[:, :], bFa[:, 0:P], ACT.Copy)
                f(oc1[:, :], bFa[0:C1, P:2 * P], ACT.Copy).then_inc(s_oc, 1)

            def Fa_x1(q):
                act.wait_ge(s_st2, q + 1)
                f(xh[:, bass.ds(q, 1), :].rearrange("p z c -> p (z c)"), bFa[:, 0:C], ACT.Copy).then_inc(s_x1, 1)

            def Fa_h(q):
                act.wait_ge(s_nm2, q + 1)
                if old(0, q if not isinstance(q, int) else q - 1):
                    act.wait_ge(s_h2Tp, q)
                f(h2[:, :], bFa[:, 0:C], ACT.Identity, scale=rstd2[:, 0:1],
                  bias=nmr2[:, 0:1]).then_inc(s_h2, 1)

            def Fa_hT(q, fp):
                act.wait_ge(s_h2Tp, q + 1)
                if old(0, q if not isinstance(q, int) else q - 1):
                    act.wait_ge(s_split, q)
                if old(0, q if not isinstance(q, int) else q - 2):
                    act.wait_ge(s_up, q * UN - UN)
                f(h2T[:, :], bFa[:, 0:2 * P], ACT.Copy)
                f(hiT[:, fp], bFa[:, 0:2 * P], ACT.Copy).then_inc(s_h2T, 1)

            def Fa_exp(q):
                act.wait_ge(s_nmx, q + 1)
                if old(0, q if not isinstance(q, int) else q - 1):
                    act.wait_ge(s_gate, q)
                f(prob[:, 0:E], bFa[:, 0:E], ACT.Exp, bias=negmax[:, 0:1])
                f(prob[:, E:E + 1], bFa[:, E:E + 1], ACT.Exp, scale=-1.0, bias=neg_sgb[:, 0:1]).then_inc(s_pr, 1)

            def weights_hi0(m):
                if m == 0:
                    act.wait_ge(s_wu[0], 4 * 16)
                f(Whi0[:, m], raw0[:, m], ACT.Copy).then_inc(s_whi, 1)

            def weights_hi1(m):
                if m == 0:
                    act.wait_ge(s_wu[1], 8 * 16)
                    act.wait_ge(s_clear, len(free))
                if m >= len(free):
                    act.wait_ge(s_w1, m - len(free) + 1)
                f(free[m % len(free)][C1:P].bitcast(F32R), raw1[C1:P, m], ACT.Copy).then_inc(s_whi, 1)

            def unit(q, fp, m):
                act.wait_ge(s_up, q * UN + (m + 1))
                if m >= RING or not isinstance(q, int) or q >= 1:
                    act.wait_ge(s_hid, q * UN + (m + 1 - RING))
                if m == 0:
                    act.wait_ge(s_gate, q + 1)
                f(sg[:, m % RING], bUp[m % 2][:, 0:H], ACT.Silu)
                f(ug[:, m % RING], bUp[m % 2][:, H:2 * H], ACT.Copy, scale=gate[:, fp, m:m + 1]).then_inc(s_ug, 1)

            def hidden(q, g):
                lo, hi = GRP[g]
                act.wait_ge(s_ht, q * NG + (g + 1))
                if g >= 2:
                    act.wait_ge(s_dg, q * NG + (g - 1))
                elif g == 0 and (not isinstance(q, int) or q >= 1):
                    act.wait_ge(s_dg, q * NG)
                w = (hi - lo) * P
                f(hidT[:, turn_bank(g)].rearrange("p k t -> p (k t)")[:, 0:w], bHt[turn_bank(g)][:, 0:w], ACT.Copy).then_inc(s_htc, 1)

            def Fc_res(q):
                act.wait_ge(s_dg, q * NG + NG)
                if old(0, q if not isinstance(q, int) else q - 1):
                    act.wait_ge(s_outp, q)
                f(res[:, :], bDn[:, 0:C], ACT.Copy).then_inc(s_res, 1)

            def Fc_out(q):
                act.wait_ge(s_outp, q + 1)
                at = q * T
                f(xT0[:, :, bass.ds(at, T)], bDn[:, 0:P].rearrange("c (b t) -> c b t", b=NB), ACT.Copy)
                f(xT1[:, :, bass.ds(at, T)], bDn[0:C1, P:2 * P].rearrange("c (b t) -> c b t", b=NB), ACT.Copy).then_inc(s_outc, 1)

            def step(c, par, on):
                X_, A, A2, R, Fa, Fb, Fc = (on.get(k) for k in ("X", "A", "A2", "R", "Fa", "Fb", "Fc"))
                if n[0]:
                    act.sem_clear(s_act)
                    n[0] = 0

                def do(q, fn, *args):
                    if q is not None:
                        fn(q, *args)

                def units(*ms):
                    for m in ms:
                        do(Fb, unit, par, m)
                        if isinstance(c, int) and c == 1:
                            weights_hi1(m)

                def hT(g):
                    do(Fb, hidden, g)

                do(A, A_h)
                do(Fc, Fc_res)
                do(R, place, par, 1)
                units(0)
                do(A, A_hT)
                units(1)
                do(A, A_silu)
                units(2)
                do(X_, A_xs)
                do(Fa, Fa_oc)
                units(3)
                do(Fc, Fc_out)
                units(4)
                hT(0)
                units(5)
                do(Fa, Fa_x1)
                units(6)
                do(Fa, Fa_h)
                do(A2, place, 1 - par, 0)
                do(Fa, Fa_hT, 1 - par)
                hT(1)
                units(7)
                do(A, A_inv)
                if isinstance(c, int) and Fa == 0:
                    act.wait_ge(s_sgb, 1)
                do(Fa, Fa_exp)
                units(8)
                hT(2)
                units(9, 10, 11)
                hT(3)
                hT(4)
                if isinstance(c, int) and c == -1:
                    for m in range(UN):
                        weights_hi0(m)

            nc.scalar.preload_act_table_set("silu_and_others")
            act.wait_ge(s_x[0], 32)
            act.wait_ge(s_const, 4)
            chunks(act, step)

        @block.gpsimd
        def _(pool):
            tt = nc.gpsimd.tensor_tensor
            n = [0]

            def chained(ins):
                n[0] += 1
                ins.then_inc(s_pool, 1)
                pool.wait_ge(s_pool, n[0])

            def rstd(a, ready, mv, ve, out_, eps, done, used):
                pool.wait_ge(ready, a + 1)
                if old(0, a if not isinstance(a, int) else a - 1):
                    pool.wait_ge(used, a)
                chained(tt(ve[:, :], mv[:, 1:2], eps[:, :], ALU.add))
                tt(out_[:, :], ve[:, :], neg_half[:, :], ALU.pow).then_inc(done, 1)

            def A_rstd(a):
                rstd(a, s_st1, mv1, ve1, rstd1, eps6, s_rs1, s_h)
                pool.wait_ge(s_rs1, a + 1)
                if old(0, a if not isinstance(a, int) else a - 1):
                    pool.wait_ge(s_xh, a)
                tt(rstd_1[:, :], rstd1[:, :], one[:, :], ALU.add).then_inc(s_rs_1, 1)

            def A_norm(a):
                pool.wait_ge(s_inv, a + 1)
                if old(0, a if not isinstance(a, int) else a - 1):
                    pool.wait_ge(s_scr, a * 128)
                    pool.wait_ge(s_vT, a)
                tt(kqn[:, 1].rearrange("p x (h d) -> p (x h) d", d=D), qk[:, 0].rearrange("p x h d -> p (x h) d"),
                   inv[:, 0:12].unsqueeze(2).to_broadcast([P, NH, D]), ALU.mult).then_inc(s_qn, 1)
                pool.wait_ge(s_vs, a + 1)
                tt(vn[:, :, :, :].rearrange("p h x d -> p (h x) d"), v[:, :, :, :].rearrange("p h x d -> p (h x) d"),
                   inv[:, 24:36].unsqueeze(2).to_broadcast([P, NH, D]), ALU.mult).then_inc(s_vn, 1)

            def products(c, half, part):
                if part == 0:
                    pool.wait_ge(s_state, c * 2 + (half + 1))
                    pool.wait_ge(s_QB[half], c * 32 + 32)
                    if half or not isinstance(c, int) or c > 0:
                        pool.wait_ge(s_oT, c * 2 + half)
                n, at = T // 4, part * (T // 4)
                lo = half * (T // 2) + at
                tt(PQ[:, at * BR * HP:(at + n) * BR * HP].rearrange("p (i b h) d -> p i b (h d)", i=n, b=BR),
                   SH[:, lo:lo + n].rearrange("p i b h d -> p i b (h d)"),
                   QB[:, :, lo:lo + n].rearrange("p b i h d -> p i b (h d)"), ALU.mult).then_inc(s_pq, 1)
                if part == 1:
                    pool.wait_ge(s_pq, c * 4 + (2 * half + 2))

            def sums(c, half, w):
                chained(tt(PQ[:, :, 0:w], PQ[:, :, 0:w], PQ[:, :, w:2 * w], ALU.add))

            def rest(c, half):
                lo = half * (T // 2)
                sums(c, half, 4)
                sums(c, half, 2)
                if half == 0 and old(0, c if not isinstance(c, int) else c - 1):
                    pool.wait_ge(s_otok, c)
                s = PQ[:, :, 0:2].rearrange("p (i b h) d -> p i b h d", i=T // 2, b=BR)
                tt(oT[:, :, :, lo:lo + T // 2].rearrange("p h b i -> p i b h"), s[:, :, :, :, 0], s[:, :, :, :, 1],
                   ALU.add).then_inc(s_oT, 1)

            def weights_lo0(m):
                pool.wait_ge(s_whi, m + 1)
                tt(Wlo0[:, m], raw0[:, m], Whi0[:, m].bitcast(F32), ALU.subtract).then_inc(s_wlo0, 1)

            def weights_1(m):
                pool.wait_ge(s_whi, UN + m + 1)
                tt(W1[:, m], raw1[:, m], free[m % len(free)], ALU.subtract).then_inc(s_w1, 1)

            def split(q, fp):
                pool.wait_ge(s_h2T, q + 1)
                tt(loT[:, fp], h2T[:, :], hiT[:, fp].bitcast(F32), ALU.subtract).then_inc(s_split, 1)

            def hidden(q, m):
                pool.wait_ge(s_ug, q * UN + (m + 1))
                if m >= UN // 2 or not isinstance(q, int) or q >= 1:
                    last = ((m - UN // 2) % UN + 1) * H - 1
                    g = [lo * P <= last < hi * P for lo, hi in GRP].index(True)
                    pool.wait_ge(s_ht, q * NG + (g + 1 - (0 if m >= UN // 2 else NG)))
                r = m % (UN // 2)
                tt(hid[:, r * H:(r + 1) * H], sg[:, m % RING], ug[:, m % RING], ALU.mult).then_inc(s_hid, 1)

            def step(c, par, on):
                X_, A2, R, Fa, Fb = (on.get(k) for k in ("X", "A2", "R", "Fa", "Fb"))
                Fo = None if isinstance(c, int) and c == NC else Fa
                if n[0]:
                    pool.sem_clear(s_pool)
                    n[0] = 0

                def do(q, fn, *args):
                    if q is not None:
                        fn(q, *args)

                def units(*ms):
                    for m in ms:
                        do(Fb, hidden, m)
                        if isinstance(c, int) and c == 1:
                            weights_1(m)

                do(A2, A_norm)
                do(Fo, products, 1, 0)
                do(Fo, products, 1, 1)
                do(Fo, sums, 1, 8)
                do(Fo, rest, 1)
                units(0, 1, 2, 3, 4)
                do(Fa, rstd, s_st2, mv2, ve2, rstd2, eps5, s_rs2, s_h2)
                units(5)
                do(R, products, 0, 0)
                do(R, products, 0, 1)
                do(Fa, split, 1 - par)
                units(6, 7)
                do(R, sums, 0, 8)
                do(X_, A_rstd)
                units(8, 9, 10)
                do(R, rest, 0)
                units(11)
                if isinstance(c, int) and c == -1:
                    for m in range(UN):
                        weights_lo0(m)

            pool.memset(ident[:, :], 0.0).then_inc(s_id, 1)
            pool.wait_ge(s_id, 1)
            pool.affine_select(out=ident[:, :], in_=ident[:, :], compare_op=ALU.not_equal, fill=1.0, base=0,
                               pattern=[[-1, P]], channel_multiplier=1).then_inc(s_id, 1)
            for t, val in ((neg_half, -0.5), (eps6, 1e-6), (eps5, 1e-5), (one, 1.0)):
                pool.memset(t[:, :], val).then_inc(s_const, 1)
            pool.memset(lower[:, :, :], 1.0).then_inc(s_low, 1)
            pool.wait_ge(s_low, 1)
            pool.affine_select(out=lower[:, :, :], in_=lower[:, :, :], compare_op=ALU.is_gt, fill=0.0, base=0,
                               pattern=[[1, E], [-1, E]], channel_multiplier=0).then_inc(s_low, 1)
            pool.memset(SH[:, T - 1], 0.0).then_inc(s_zero, 1)
            for b in free:
                pool.memset(b, 0.0).then_inc(s_clear, 1)
            pool.wait_ge(s_const, 4)
            chunks(pool, step)

        @block.vector
        def _(dve):
            tt, ts = nc.vector.tensor_tensor, nc.vector.tensor_scalar
            n = [0]

            def count(ins):
                n[0] += 1
                ins.then_inc(s_chain, 1)
                return s_chain, n[0]

            def stats(src, st, mv, done):
                dve.wait_ge(*count(nc.vector.bn_stats(st[:, :], src)))
                nc.vector.bn_aggr(mv[:, :], st[:, :]).then_inc(done, 1)

            def A_stats(a):
                dve.wait_ge(s_xT, a + 1)
                if old(0, a if not isinstance(a, int) else a - 1):
                    dve.wait_ge(s_rs1, a)
                    dve.wait_ge(s_nm1, a)
                stats(bA[:, 0:C], st1, mv1, s_st1)

            def nmr(a, mv, rs, out_, rs_ready, used, done):
                dve.wait_ge(rs_ready, a + 1)
                if old(0, a if not isinstance(a, int) else a - 1):
                    dve.wait_ge(used, a)
                nc.vector.scalar_tensor_tensor(out=out_[:, :], in0=mv[:, 0:1], scalar=-1.0, in1=rs[:, :], op0=ALU.mult,
                                               op1=ALU.mult).then_inc(done, 1)

            def A_z(a):
                dve.wait_ge(s_vb, a + 1)
                if old(0, a if not isinstance(a, int) else a - 1):
                    dve.wait_ge(s_inv, a)
                ts(zc[:, :], bA[:, C:C + NH], -40.0, None, ALU.max).then_inc(s_z, 1)

            def A_ss(a):
                dve.wait_ge(s_sq, a + 1)
                if old(0, a if not isinstance(a, int) else a - 1):
                    dve.wait_ge(s_inv, a)
                nc.vector.tensor_reduce(ss[:, :], sq[:, :, :, :, :].rearrange("p t x h d -> p (t x h) d"), X, ALU.add).then_inc(s_ss, 1)

            def A_kn(a):
                dve.wait_ge(s_inv, a + 1)
                if old(0, a if not isinstance(a, int) else a - 1):
                    dve.wait_ge(s_scr, a * 128)
                w = count(tt(ksc[:, :, :], inv[:, 12:24].rearrange("p (x h) -> p x h", x=HX),
                             inv[:, 24:36].rearrange("p (h x) -> p x h", x=HX), ALU.mult))
                dve.wait_ge(*w)
                tt(kqn[:, 0].rearrange("p x (h d) -> p (x h) d", d=D), qk[:, 1].rearrange("p x h d -> p (x h) d"),
                   ksc[:, :, :].rearrange("p x h -> p (x h)").unsqueeze(2).to_broadcast([P, NH, D]), ALU.mult).then_inc(s_kn, 1)

            def A_vT(a, par):
                dve.wait_ge(s_vn, a + 1)
                if old(0, a if not isinstance(a, int) else a - 2):
                    dve.wait_ge(s_place, a * 2 - 2)
                nc.vector.transpose(vT[:, par].rearrange("p h b i -> p (h b i)"), vn[:, :, :, :].rearrange("p h x d -> p (h x d)")).then_inc(s_vT, 1)

            def Fa_otok(q):
                dve.wait_ge(s_oT, q * 2 + 2)
                if old(0, q if not isinstance(q, int) else q - 1):
                    dve.wait_ge(s_ocp, q)
                nc.vector.transpose(otok[:, :], oT[:, :, :, :].rearrange("p h b i -> p (h b i)")).then_inc(s_otok, 1)

            def last_out():
                dve.wait_ge(s_QB[1], NC * 32)
                dve.wait_ge(s_oT, 2 * NC - 1)
                w = count(tt(PQ[:, :, :].rearrange("p (i b h) d -> p i b (h d)", i=T // 2, b=BR),
                             SH[:, T // 2:T].rearrange("p i b h d -> p i b (h d)"),
                             QB[:, :, T // 2:T].rearrange("p b i h d -> p i b (h d)"), ALU.mult))
                for n in (8, 4, 2):
                    dve.wait_ge(*w)
                    w = count(tt(PQ[:, :, 0:n], PQ[:, :, 0:n], PQ[:, :, n:2 * n], ALU.add))
                dve.wait_ge(*w)
                two = PQ[:, :, 0:2].rearrange("p (i b h) d -> p i b h d", i=T // 2, b=BR)
                tt(oT[:, :, :, T // 2:T].rearrange("p h b i -> p i b h"), two[:, :, :, :, 0], two[:, :, :, :, 1],
                   ALU.add).then_inc(s_oT, 1)

            def Fa_stats(q):
                dve.wait_ge(s_y, q + 1)
                if old(0, q if not isinstance(q, int) else q - 1):
                    dve.wait_ge(s_rs2, q)
                    dve.wait_ge(s_nm2, q)
                stats(bFa[:, 0:C], st2, mv2, s_st2)

            def Fa_max(q):
                dve.wait_ge(s_lg, q + 1)
                nc.vector.tensor_reduce(negmax[:, :], bFa[:, 0:E], X, ALU.max, negate=True).then_inc(s_nmx, 1)

            def Fa_gates(q, fp):
                pe_, po = prob[:, 0:E].unsqueeze(2).to_broadcast([P, E, E]), prob[:, 0:E].unsqueeze(1).to_broadcast([P, E, E])
                w = {}
                def rank1():
                    dve.wait_ge(s_pr, q + 1)
                    if old(0, q if not isinstance(q, int) else q - 2):
                        dve.wait_ge(s_ug, q * UN - UN)
                    w["dif"] = count(tt(gt[:, :, :], po, pe_, ALU.subtract))
                    count(ts(den[:, 1:2], prob[:, E:E + 1], 1.0, None, ALU.add))
                def rank2():
                    dve.wait_ge(*w["dif"])
                    w["eq"] = count(nc.vector.scalar_tensor_tensor(out=eq[:, :, :], in0=gt[:, :, :], scalar=0.0, in1=lower[:, :, :],
                                                                   op0=ALU.is_equal, op1=ALU.mult))
                def rank3():
                    dve.wait_ge(*w["eq"])
                    w["gt"] = count(nc.vector.scalar_tensor_tensor(out=gt[:, :, :], in0=gt[:, :, :], scalar=0.0, in1=eq[:, :, :],
                                                                   op0=ALU.is_gt, op1=ALU.add))
                def rank4():
                    dve.wait_ge(*w["gt"])
                    w["rank"] = count(nc.vector.tensor_reduce(rank[:, :], gt[:, :, :], X, ALU.add))
                def pick():
                    dve.wait_ge(*w["rank"])
                    w["sel"] = count(nc.vector.scalar_tensor_tensor(out=sel[:, :], in0=rank[:, :], scalar=2.0, in1=prob[:, 0:E],
                                                                    op0=ALU.is_lt, op1=ALU.mult))
                def total():
                    dve.wait_ge(*w["sel"])
                    w["den"] = count(nc.vector.tensor_reduce(den[:, 0:1], sel[:, :], X, ALU.add))
                def recip():
                    dve.wait_ge(*w["den"])
                    w["rden"] = count(nc.vector.reciprocal(rden[:, :], den[:, :]))
                def coefs():
                    dve.wait_ge(*w["rden"])
                    w["om"] = count(ts(coef[:, :], rden[:, 1:2], -1.0, 1.0, ALU.mult, ALU.add))
                    count(ts(gate[:, fp, E:UN], one[:, 0:1].to_broadcast([P, UN - E]), rden[:, 1:2], None, ALU.mult))
                def coef2():
                    dve.wait_ge(*w["om"])
                    w["co"] = count(tt(coef[:, :], coef[:, :], rden[:, 0:1], ALU.mult))
                def last():
                    dve.wait_ge(*w["co"])
                    ts(gate[:, fp, 0:E], sel[:, :], coef[:, 0:1], None, ALU.mult).then_inc(s_gate, 1)
                return [rank1, rank2, rank3, rank4, pick, total, recip, coefs, coef2, last]

            def negate_sgb():
                dve.wait_ge(s_wr, 80)
                ts(neg_sgb[:, :], sgb[:, :], -1.0, None, ALU.mult).then_inc(s_sgb, 1)

            def step(c, par, on):
                X_, A, A2, R, Fa, Fb, Fc = (on.get(k) for k in ("X", "A", "A2", "R", "Fa", "Fb", "Fc"))
                gates = Fa_gates(Fa, 1 - par) if Fa is not None else []

                def others(done):
                    def after(n, q, fn, *args):
                        if done == n and q is not None:
                            fn(q, *args)

                    if done == 0 and isinstance(c, int) and c == NC:
                        last_out()
                    after(16, A2, A_kn)
                    after(22, A2, A_vT, 1 - par)
                    after(24, A, A_z)
                    after(26, Fa, Fa_otok)
                    after(34, Fa, Fa_stats)
                    after(39, Fa, nmr, mv2, rstd2, nmr2, s_rs2, s_h2, s_nm2)
                    after(41, A, A_ss)
                    after(48, X_, A_stats)
                    after(50, Fa, Fa_max)
                    if 0 <= done - 54 < len(gates):
                        gates[done - 54]()
                    if done == 63 and isinstance(c, int) and c == 0:
                        negate_sgb()
                    after(64, X_, nmr, mv1, rstd1, nmr1, s_rs1, s_xh, s_nm1)

                if R is None:
                    for k in range(4 * T):
                        others(k)
                if R is not None:
                    Sb = [None, None]
                    for i in range(T):
                        prev = SH[:, (i - 1) % T]
                        slot = 4 * i
                        if i % (T // 2) == 0:
                            dve.wait_ge(s_KB[i // (T // 2)], c * 32 + 32)
                            dve.wait_ge(s_place, c * 2 + (i // (T // 2) + 1))
                            if not isinstance(c, int) or c >= 1:
                                dve.wait_ge(s_pq, c * 4 - 2 + 2 * (i // (T // 2)))
                        def each(fn, waits):
                            got = []
                            for br in range(BR):
                                if waits[br] is not None:
                                    dve.wait_ge(*waits[br])
                                got.append(fn(br))
                            return got
                        w = each(lambda br: count(tt(Pr[:, br, i, :, 0:D], prev[:, br], KB[:, br, i], ALU.mult)), Sb)
                        others(slot)
                        w = each(lambda br: count(nc.vector.tensor_reduce(u[:, i % 2, br], Pr[:, br, i], X, ALU.add, negate=True)), w)
                        others(slot + 1)
                        w = each(lambda br: count(tt(TT[:, i % 2, br], KB[:, br, i],
                                                     u[:, i % 2, br].unsqueeze(2).to_broadcast([P, HP, D]), ALU.mult)), w)
                        others(slot + 2)
                        def grow(br):
                            ins = tt(SH[:, i, br], prev[:, br], TT[:, i % 2, br], ALU.add)
                            if i % (T // 2) == T // 2 - 1 and br == BR - 1:
                                ins.then_inc(s_state, 1)
                                return s_state, c * 2 + (i // (T // 2) + 1)
                            return count(ins)
                        Sb = each(grow, w)
                        others(slot + 3)
                others(4 * T)
                if n[0]:
                    dve.wait_ge(s_chain, n[0])
                if R is not None:
                    dve.wait_ge(s_state, c * 2 + 2)
                if n[0]:
                    dve.sem_clear(s_chain)
                n[0] = 0

            dve.wait_ge(s_const, 4)
            dve.wait_ge(s_low, 2)
            dve.wait_ge(s_zero, 1)
            chunks(dve, step)


_INS = ['x', 'L0_conv_Wq', 'L0_conv_Wk', 'L0_conv_Wv', 'L0_conv_Wb', 'L0_conv_Wo', 'L0_ffn_router_w', 'L0_ffn_w_gate',
        'L0_ffn_w_up', 'L0_ffn_w_down', 'L0_ffn_ws_gate', 'L0_ffn_ws_up', 'L0_ffn_ws_down', 'L0_ffn_sg_w', 'L0_ffn_sg_b']


def kernel(**inputs):
    import numpy as _np
    import concourse.bacc as _bacc
    from concourse import mybir as _mybir
    from concourse.bass_utils import run_bass_kernel_spmd as _run

    nc = _bacc.Bacc("TRN2", target_bir_lowering=False, num_devices=1)
    arrays, args = {}, []
    for name in _INS:
        a = _np.ascontiguousarray(inputs[name])
        shape = (NB, C, L) if name == 'x' else a.shape
        a = a.reshape(shape)
        arrays[f"in_{name}_dram"] = a
        args.append(nc.dram_tensor(f"in_{name}_dram", a.shape, _mybir.dt.from_np(a.dtype), kind="ExternalInput").ap())
    o = nc.dram_tensor("out_0_dram", (NB, C, L), _mybir.dt.float32, kind="ExternalOutput").ap()
    build(nc, *args, o)
    r = _run(nc, [arrays], core_ids=[0])
    return r.results[0]["out_0_dram"].reshape(NB, C, 16, 16)
```
